# Optimizing a Trainium2 kernel written in Bass

```python
import numpy as np
import jax
import jax.numpy as jnp

def _softmax(x, axis=-1):
    return jax.nn.softmax(x, axis=axis)

def _gelu(x):
    return jax.nn.gelu(x, approximate=True)

def _silu(x):
    return jax.nn.silu(x)

def _sigmoid(x):
    return jax.nn.sigmoid(x)

def _layernorm(x, axis=-1, eps=1e-05):
    m = jnp.mean(x, axis=axis, keepdims=True)
    v = jnp.var(x, axis=axis, keepdims=True)
    return (x - m) / jnp.sqrt(v + eps)

def _scatter_add(tgt, idx, src, axis=0):
    return tgt.at[idx].add(src)

def _segment_sum(src, seg, n):
    return jax.ops.segment_sum(src, seg, n)
kernel_name = 'mk_flamingo_gated_d4_seqx_r8_adbfaa'

def setup_inputs(seed: int=0):
    np.random.seed(seed)
    _w = jnp.asarray

    def _rec_inputs():
        import jax
        import jax.numpy as jnp
        _rk = jax.random.key(seed)
        x = -0.0002928 + 1 * jax.random.normal(jax.random.fold_in(_rk, 1), (8, 256, 128), jnp.float32)
        _lenS = 256 - jax.random.randint(jax.random.fold_in(_rk, 7), (8,), 0, max(1, 256 // 4) + 1, jnp.int32)
        _lenS2 = 256 - jax.random.randint(jax.random.fold_in(_rk, 8), (8,), 0, max(1, 256 // 4) + 1, jnp.int32)
        _ctx_1024P = jax.random.normal(jax.random.fold_in(_rk, 11), (8, 16, 128), jnp.float32)
        _ctx_1024c = jax.random.dirichlet(jax.random.fold_in(_rk, 511), 0.3 * jnp.ones((16,), jnp.float32), (8, 256))
        _ctx_1024t = jnp.einsum('bsk,bkd->bsd', _ctx_1024c, _ctx_1024P)
        _ctx_1024t = _ctx_1024t * jax.lax.rsqrt(jnp.mean(jnp.square(_ctx_1024t)) + 1e-12) * 0.953939
        ctx_1024 = -1.39393e-06 + 0.999914 * (_ctx_1024t + 0.3 * jax.random.normal(jax.random.fold_in(_rk, 611), (8, 256, 128), jnp.float32))
        _g = jax.random.normal(jax.random.fold_in(_rk, 9001), (2, 4), jnp.float32)
        _g = jnp.sign(_g) * jnp.maximum(jnp.abs(_g), 1.0) + (_g == 0) * 1.0
        g_xattn = _g[0]
        g_ffn = _g[1]
        return (x, ctx_1024, g_xattn, g_ffn)
    x, ctx_1024, g_xattn, g_ffn = _rec_inputs()

    def _L0_xattn_setup():
        import jax, jax.numpy as jnp
        import numpy as np
        B, S, E, NH = (2, 256, 128, 4)
        HD = E // NH

        def _mlstm_head(q, k, v, ig, fg, eps=1e-06):
            s, dh = q.shape
            log_f = jax.nn.log_sigmoid(fg)
            cs = jnp.concatenate([jnp.zeros((1, 1), log_f.dtype), jnp.cumsum(log_f, axis=0)], axis=0)
            neg = jnp.asarray(-0.7 * jnp.finfo(cs.dtype).max, cs.dtype)
            log_d = jnp.where(jnp.tri(s, dtype=bool), (cs - cs.T)[1:, 1:] + ig.T, neg)
            m = jnp.max(log_d, axis=-1, keepdims=True)
            d = jnp.exp(log_d - m)
            c = q @ (k.T / jnp.sqrt(dh)) * d
            n = jnp.maximum(jnp.sum(c, axis=-1, keepdims=True), jnp.exp(-m))
            return c / (n + eps) @ v
        key = jax.random.key(seed)
        ks = jax.random.split(key, 8)
        return {'q': jax.random.normal(ks[0], (B, S, E), jnp.float32), 'k': jax.random.normal(ks[1], (B, S, E), jnp.float32), 'v': jax.random.normal(ks[2], (B, S, E), jnp.float32), 'igate_kernel': jax.random.normal(ks[3], (3 * E, NH), jnp.float32) * 0.02, 'igate_bias': jax.random.normal(ks[4], (NH,), jnp.float32) * 0.1, 'fgate_kernel': jax.random.normal(ks[5], (3 * E, NH), jnp.float32) * 0.02, 'fgate_bias': jnp.linspace(3.0, 6.0, NH, dtype=jnp.float32), 'rms_scale': jax.random.normal(ks[6], (HD,), jnp.float32) * 0.02}
    _L0_xattn_all = _L0_xattn_setup()
    _L0_xattn_in = {k: v for k, v in _L0_xattn_all.items() if k in ('igate_kernel', 'igate_bias', 'fgate_kernel', 'fgate_bias', 'rms_scale')}
    del _L0_xattn_all

    def _L0_ffn_setup():
        import jax, jax.numpy as jnp
        import numpy as np
        D_MODEL = 128
        D_FF = 512
        N_EXPERTS = 8
        TOP_K = 2
        LN_EPS = 1e-06

        def _moe(x, router_w, w1, b1, w2, b2, gamma, beta):
            B, S, D = x.shape
            x_flat = x.reshape(-1, D)
            N = x_flat.shape[0]
            logits = x_flat @ router_w
            gate_vals, gate_idx = jax.lax.top_k(logits, TOP_K)
            gate_w = jax.nn.softmax(gate_vals, axis=-1)
            gates = jnp.zeros_like(logits).at[jnp.arange(N)[:, None], gate_idx].set(gate_w)
            h = jax.nn.gelu(jnp.einsum('nd,edf->enf', x_flat, w1) + b1[:, None, :], approximate=False)
            out = jnp.einsum('enf,efd->end', h, w2) + b2[:, None, :]
            res = x_flat[None, :, :] + out
            mu = jnp.mean(res, axis=-1, keepdims=True)
            var = jnp.mean(jnp.square(res - mu), axis=-1, keepdims=True)
            normed = (res - mu) * jax.lax.rsqrt(var + LN_EPS)
            expert_out = normed * gamma[:, None, :] + beta[:, None, :]
            y = jnp.einsum('end,ne->nd', expert_out, gates)
            return y.reshape(B, S, D)
        key = jax.random.key(seed)
        ks = jax.random.split(key, 8)
        x = jax.random.normal(ks[0], (2, 256, D_MODEL), dtype=jnp.float32)
        router_w = jax.random.normal(ks[1], (D_MODEL, N_EXPERTS), dtype=jnp.float32) * 0.02
        w1 = jax.random.normal(ks[2], (N_EXPERTS, D_MODEL, D_FF), dtype=jnp.float32) * 0.02
        b1 = jnp.zeros((N_EXPERTS, D_FF), dtype=jnp.float32)
        w2 = jax.random.normal(ks[3], (N_EXPERTS, D_FF, D_MODEL), dtype=jnp.float32) * 0.02
        b2 = jnp.zeros((N_EXPERTS, D_MODEL), dtype=jnp.float32)
        gamma = jnp.ones((N_EXPERTS, D_MODEL), dtype=jnp.float32)
        beta = jnp.zeros((N_EXPERTS, D_MODEL), dtype=jnp.float32)
        return {'x': x, 'router_w': router_w, 'w1': w1, 'b1': b1, 'w2': w2, 'b2': b2, 'gamma': gamma, 'beta': beta}
    _L0_ffn_all = _L0_ffn_setup()
    _L0_ffn_in = {k: v for k, v in _L0_ffn_all.items() if k in ('router_w', 'w1', 'b1', 'w2', 'b2', 'gamma', 'beta')}
    del _L0_ffn_all

    def _L1_xattn_setup():
        import jax, jax.numpy as jnp
        import numpy as np
        EMBED_DIM = 128
        NUM_HEADS = 16
        HEAD_DIM = EMBED_DIM // NUM_HEADS

        def _xavier_uniform(key, out_dim, in_dim):
            limit = jnp.sqrt(6.0 / (in_dim + out_dim)).astype(jnp.float32)
            return jax.random.uniform(key, (out_dim, in_dim), jnp.float32, -limit, limit)
        key = jax.random.key(seed)
        ks = jax.random.split(key, 6)
        B, S, D = (4, 256, EMBED_DIM)
        return {'query': jax.random.normal(ks[0], (B, S, D), jnp.float32), 'key': jax.random.normal(ks[1], (B, S, D), jnp.float32), 'value': jax.random.normal(ks[2], (B, S, D), jnp.float32), 'Wq': _xavier_uniform(ks[3], D, D), 'Wk': _xavier_uniform(ks[4], D, D), 'Wv': _xavier_uniform(ks[5], D, D)}
    _L1_xattn_all = _L1_xattn_setup()
    _L1_xattn_in = {k: v for k, v in _L1_xattn_all.items() if k in ('Wq', 'Wk', 'Wv')}
    del _L1_xattn_all

    def _L1_ffn_setup():
        import jax, jax.numpy as jnp
        import numpy as np
        TOPK = 4
        key = jax.random.key(seed)
        ks = jax.random.split(key, 9)
        B, T, D = (4, 256, 128)
        E, H = (32, 128)
        HS = H * TOPK
        s = lambda k, shape, fan: jax.random.normal(k, shape, dtype=jnp.float32) / np.sqrt(fan)
        return {'x': jax.random.normal(ks[0], (B, T, D), dtype=jnp.float32), 'router_w': s(ks[1], (E, D), D), 'router_bias': jnp.zeros((E,), dtype=jnp.float32), 'gate_w': s(ks[2], (E, H, D), D), 'up_w': s(ks[3], (E, H, D), D), 'down_w': s(ks[4], (E, D, H), H), 'sgate_w': s(ks[5], (HS, D), D), 'sup_w': s(ks[6], (HS, D), D), 'sdown_w': s(ks[7], (D, HS), HS)}
    _L1_ffn_all = _L1_ffn_setup()
    _L1_ffn_in = {k: v for k, v in _L1_ffn_all.items() if k in ('router_w', 'router_bias', 'gate_w', 'up_w', 'down_w', 'sgate_w', 'sup_w', 'sdown_w')}
    del _L1_ffn_all

    def _L2_xattn_setup():
        import jax, jax.numpy as jnp
        import numpy as np
        N_HEAD = 16
        key = jax.random.key(seed)
        ks = jax.random.split(key, 5)
        b, l, d = (4, 256, 128)
        dh = d // N_HEAD
        return {'q': jax.random.normal(ks[0], (b, l, d), dtype=jnp.float32), 'kv': jax.random.normal(ks[1], (b, l, d), dtype=jnp.float32), 'Wq': jax.random.normal(ks[2], (d, d), dtype=jnp.float32) * 0.02, 'Wkv': jax.random.normal(ks[3], (2 * dh, d), dtype=jnp.float32) * 0.02, 'Wc': jax.random.normal(ks[4], (d, d), dtype=jnp.float32) * 0.02}
    _L2_xattn_all = _L2_xattn_setup()
    _L2_xattn_in = {k: v for k, v in _L2_xattn_all.items() if k in ('Wq', 'Wkv', 'Wc')}
    del _L2_xattn_all

    def _L2_ffn_setup():
        import jax, jax.numpy as jnp
        import numpy as np
        import math
        D = 128
        H = 16
        E = 8
        TOPK = 2
        LAT = D // 2
        KPH = LAT // H
        HD = D // H

        def _forward(hs, q_w, q_b, k_w, k_b, v_w, v_b, o_w, o_b, router_w, router_b, w1, b1, w2, b2):
            B, S, _ = hs.shape
            Q = (hs @ q_w + q_b).reshape(B, S, H, HD).transpose(0, 2, 1, 3)
            K = (hs @ k_w + k_b).reshape(B, S, H, KPH).transpose(0, 2, 1, 3)
            V = (hs @ v_w + v_b).reshape(B, S, H, KPH).transpose(0, 2, 1, 3)
            scores = jnp.einsum('bhsk,bhtk->bhst', Q[..., :KPH], K) / math.sqrt(KPH)
            attn = jax.nn.softmax(scores, axis=-1)
            ao = jnp.einsum('bhst,bhtv->bhsv', attn, V)
            ao = ao.transpose(0, 2, 1, 3).reshape(B, S, H * KPH)
            ao = jnp.concatenate([ao, jnp.zeros((B, S, D - LAT), ao.dtype)], axis=-1)
            mla_out = ao @ o_w + o_b
            probs = jax.nn.softmax(mla_out @ router_w + router_b, axis=-1)
            topw, topi = jax.lax.top_k(probs, TOPK)
            topw = topw / (topw.sum(-1, keepdims=True) + 1e-08)
            combine = jnp.sum(jax.nn.one_hot(topi, E, dtype=probs.dtype) * topw[..., None], axis=-2)
            h1 = jnp.einsum('bsd,edf->ebsf', mla_out, w1) + b1[:, None, None, :]
            h1 = jax.nn.gelu(h1, approximate=False)
            h2 = jnp.einsum('ebsf,efd->ebsd', h1, w2) + b2[:, None, None, :]
            moe_out = jnp.einsum('bse,ebsd->bsd', combine, h2)
            return hs + 0.3 * moe_out
        key = jax.random.key(seed)
        ks = jax.random.split(key, 16)
        s = 0.02
        inp = {'hidden_states': jax.random.normal(ks[0], (2, 256, D), jnp.float32), 'q_w': jax.random.normal(ks[1], (D, D), jnp.float32) * s, 'q_b': jnp.zeros((D,), jnp.float32), 'k_w': jax.random.normal(ks[2], (D, LAT), jnp.float32) * s, 'k_b': jnp.zeros((LAT,), jnp.float32), 'v_w': jax.random.normal(ks[3], (D, LAT), jnp.float32) * s, 'v_b': jnp.zeros((LAT,), jnp.float32), 'o_w': jax.random.normal(ks[4], (D, D), jnp.float32) * s, 'o_b': jnp.zeros((D,), jnp.float32), 'router_w': jax.random.normal(ks[5], (D, E), jnp.float32) * s, 'router_b': jnp.zeros((E,), jnp.float32), 'w1': jax.random.normal(ks[6], (E, D, 2 * D), jnp.float32) * s, 'b1': jnp.zeros((E, 2 * D), jnp.float32), 'w2': jax.random.normal(ks[7], (E, 2 * D, D), jnp.float32) * s, 'b2': jnp.zeros((E, D), jnp.float32)}
        return inp
    _L2_ffn_all = _L2_ffn_setup()
    _L2_ffn_in = {k: v for k, v in _L2_ffn_all.items() if k in ('q_w', 'q_b', 'k_w', 'k_b', 'v_w', 'v_b', 'o_w', 'o_b', 'router_w', 'router_b', 'w1', 'b1', 'w2', 'b2')}
    del _L2_ffn_all

    def _L3_xattn_setup():
        import jax, jax.numpy as jnp
        import numpy as np
        EMBED_DIM = 128
        NUM_HEADS = 16
        B, SQ, SK = (4, 256, 256)
        key = jax.random.key(seed)
        ks = jax.random.split(key, 5)
        scale = 1.0 / np.sqrt(EMBED_DIM)
        return {'q': jax.random.normal(ks[0], (B, SQ, EMBED_DIM), dtype=jnp.float32), 'v': jax.random.normal(ks[1], (B, SK, EMBED_DIM), dtype=jnp.float32), 'Wq': jax.random.normal(ks[2], (EMBED_DIM, EMBED_DIM), dtype=jnp.float32) * scale, 'bq': jnp.zeros((EMBED_DIM,), dtype=jnp.float32), 'Wk': jax.random.normal(ks[3], (EMBED_DIM, EMBED_DIM), dtype=jnp.float32) * scale, 'bk': jnp.zeros((EMBED_DIM,), dtype=jnp.float32), 'Wv': jax.random.normal(ks[4], (EMBED_DIM, EMBED_DIM), dtype=jnp.float32) * scale, 'bv': jnp.zeros((EMBED_DIM,), dtype=jnp.float32)}
    _L3_xattn_all = _L3_xattn_setup()
    _L3_xattn_in = {k: v for k, v in _L3_xattn_all.items() if k in ('Wq', 'bq', 'Wk', 'bk', 'Wv', 'bv')}
    del _L3_xattn_all

    def _L3_ffn_setup():
        import jax, jax.numpy as jnp
        import numpy as np
        E = 8
        K = 2
        D = 128
        H = 128
        B, T = (2, 128)
        key = jax.random.key(seed)
        ks = jax.random.split(key, 6)
        s = 0.02
        return {'x': jax.random.normal(ks[0], (B, T, D), dtype=jnp.float32), 'gate_w': jax.random.normal(ks[1], (E, D), dtype=jnp.float32) * s, 'lb_bias': jnp.zeros((E,), dtype=jnp.float32), 'w1': jax.random.normal(ks[2], (E, H, D), dtype=jnp.float32) * s, 'w2': jax.random.normal(ks[3], (E, D, H), dtype=jnp.float32) * s, 'cfc': jax.random.normal(ks[4], (H, D), dtype=jnp.float32) * s, 'cproj': jax.random.normal(ks[5], (D, H), dtype=jnp.float32) * s}
    _L3_ffn_all = _L3_ffn_setup()
    _L3_ffn_in = {k: v for k, v in _L3_ffn_all.items() if k in ('gate_w', 'lb_bias', 'w1', 'w2', 'cfc', 'cproj')}
    del _L3_ffn_all
    return {'x': x, 'ctx_1024': ctx_1024, 'g_xattn': g_xattn, 'g_ffn': g_ffn, 'L0_xattn_igate_kernel': _L0_xattn_in['igate_kernel'], 'L0_xattn_igate_bias': _L0_xattn_in['igate_bias'], 'L0_xattn_fgate_kernel': _L0_xattn_in['fgate_kernel'], 'L0_xattn_fgate_bias': _L0_xattn_in['fgate_bias'], 'L0_xattn_rms_scale': _L0_xattn_in['rms_scale'], 'L0_ffn_router_w': _L0_ffn_in['router_w'], 'L0_ffn_w1': _L0_ffn_in['w1'], 'L0_ffn_b1': _L0_ffn_in['b1'], 'L0_ffn_w2': _L0_ffn_in['w2'], 'L0_ffn_b2': _L0_ffn_in['b2'], 'L0_ffn_gamma': _L0_ffn_in['gamma'], 'L0_ffn_beta': _L0_ffn_in['beta'], 'L1_xattn_Wq': _L1_xattn_in['Wq'], 'L1_xattn_Wk': _L1_xattn_in['Wk'], 'L1_xattn_Wv': _L1_xattn_in['Wv'], 'L1_ffn_router_w': _L1_ffn_in['router_w'], 'L1_ffn_router_bias': _L1_ffn_in['router_bias'], 'L1_ffn_gate_w': _L1_ffn_in['gate_w'], 'L1_ffn_up_w': _L1_ffn_in['up_w'], 'L1_ffn_down_w': _L1_ffn_in['down_w'], 'L1_ffn_sgate_w': _L1_ffn_in['sgate_w'], 'L1_ffn_sup_w': _L1_ffn_in['sup_w'], 'L1_ffn_sdown_w': _L1_ffn_in['sdown_w'], 'L2_xattn_Wq': _L2_xattn_in['Wq'], 'L2_xattn_Wkv': _L2_xattn_in['Wkv'], 'L2_xattn_Wc': _L2_xattn_in['Wc'], 'L2_ffn_q_w': _L2_ffn_in['q_w'], 'L2_ffn_q_b': _L2_ffn_in['q_b'], 'L2_ffn_k_w': _L2_ffn_in['k_w'], 'L2_ffn_k_b': _L2_ffn_in['k_b'], 'L2_ffn_v_w': _L2_ffn_in['v_w'], 'L2_ffn_v_b': _L2_ffn_in['v_b'], 'L2_ffn_o_w': _L2_ffn_in['o_w'], 'L2_ffn_o_b': _L2_ffn_in['o_b'], 'L2_ffn_router_w': _L2_ffn_in['router_w'], 'L2_ffn_router_b': _L2_ffn_in['router_b'], 'L2_ffn_w1': _L2_ffn_in['w1'], 'L2_ffn_b1': _L2_ffn_in['b1'], 'L2_ffn_w2': _L2_ffn_in['w2'], 'L2_ffn_b2': _L2_ffn_in['b2'], 'L3_xattn_Wq': _L3_xattn_in['Wq'], 'L3_xattn_bq': _L3_xattn_in['bq'], 'L3_xattn_Wk': _L3_xattn_in['Wk'], 'L3_xattn_bk': _L3_xattn_in['bk'], 'L3_xattn_Wv': _L3_xattn_in['Wv'], 'L3_xattn_bv': _L3_xattn_in['bv'], 'L3_ffn_gate_w': _L3_ffn_in['gate_w'], 'L3_ffn_lb_bias': _L3_ffn_in['lb_bias'], 'L3_ffn_w1': _L3_ffn_in['w1'], 'L3_ffn_w2': _L3_ffn_in['w2'], 'L3_ffn_cfc': _L3_ffn_in['cfc'], 'L3_ffn_cproj': _L3_ffn_in['cproj']}

def reference(x, ctx_1024, g_xattn, g_ffn, L0_xattn_igate_kernel, L0_xattn_igate_bias, L0_xattn_fgate_kernel, L0_xattn_fgate_bias, L0_xattn_rms_scale, L0_ffn_router_w, L0_ffn_w1, L0_ffn_b1, L0_ffn_w2, L0_ffn_b2, L0_ffn_gamma, L0_ffn_beta, L1_xattn_Wq, L1_xattn_Wk, L1_xattn_Wv, L1_ffn_router_w, L1_ffn_router_bias, L1_ffn_gate_w, L1_ffn_up_w, L1_ffn_down_w, L1_ffn_sgate_w, L1_ffn_sup_w, L1_ffn_sdown_w, L2_xattn_Wq, L2_xattn_Wkv, L2_xattn_Wc, L2_ffn_q_w, L2_ffn_q_b, L2_ffn_k_w, L2_ffn_k_b, L2_ffn_v_w, L2_ffn_v_b, L2_ffn_o_w, L2_ffn_o_b, L2_ffn_router_w, L2_ffn_router_b, L2_ffn_w1, L2_ffn_b1, L2_ffn_w2, L2_ffn_b2, L3_xattn_Wq, L3_xattn_bq, L3_xattn_Wk, L3_xattn_bk, L3_xattn_Wv, L3_xattn_bv, L3_ffn_gate_w, L3_ffn_lb_bias, L3_ffn_w1, L3_ffn_w2, L3_ffn_cfc, L3_ffn_cproj):
    import jax
    import jax.numpy as jnp

    def _L0_xattn_ref(q, k, v, igate_kernel, igate_bias, fgate_kernel, fgate_bias, rms_scale):
        import jax, jax.numpy as jnp
        import numpy as np
        B, S, E, NH = (2, 256, 128, 4)
        HD = E // NH

        def _mlstm_head(q, k, v, ig, fg, eps=1e-06):
            s, dh = q.shape
            log_f = jax.nn.log_sigmoid(fg)
            cs = jnp.concatenate([jnp.zeros((1, 1), log_f.dtype), jnp.cumsum(log_f, axis=0)], axis=0)
            neg = jnp.asarray(-0.7 * jnp.finfo(cs.dtype).max, cs.dtype)
            log_d = jnp.where(jnp.tri(s, dtype=bool), (cs - cs.T)[1:, 1:] + ig.T, neg)
            m = jnp.max(log_d, axis=-1, keepdims=True)
            d = jnp.exp(log_d - m)
            c = q @ (k.T / jnp.sqrt(dh)) * d
            n = jnp.maximum(jnp.sum(c, axis=-1, keepdims=True), jnp.exp(-m))
            return c / (n + eps) @ v
        b, s, e = q.shape
        nh = igate_kernel.shape[1]
        hd = e // nh
        gate_in = jnp.concatenate((q, k, v), axis=-1)
        ig = (gate_in @ igate_kernel + igate_bias).swapaxes(-1, -2)[..., None]
        fg = (gate_in @ fgate_kernel + fgate_bias).swapaxes(-1, -2)[..., None]
        qh = q.reshape(b, s, nh, hd).swapaxes(1, 2)
        kh = k.reshape(b, s, nh, hd).swapaxes(1, 2)
        vh = v.reshape(b, s, nh, hd).swapaxes(1, 2)
        h = jax.vmap(jax.vmap(_mlstm_head))(qh, kh, vh, ig, fg)
        var = jnp.mean(jnp.square(h.astype(jnp.float32)), axis=-1, keepdims=True)
        h = (h * jax.lax.rsqrt(var + 1e-06)).astype(h.dtype) * (1.0 + rms_scale)
        return h.swapaxes(1, 2).reshape(b, s, e)

    def _L0_ffn_ref(x, router_w, w1, b1, w2, b2, gamma, beta):
        import jax, jax.numpy as jnp
        import numpy as np
        D_MODEL = 128
        D_FF = 512
        N_EXPERTS = 8
        TOP_K = 2
        LN_EPS = 1e-06

        def _moe(x, router_w, w1, b1, w2, b2, gamma, beta):
            B, S, D = x.shape
            x_flat = x.reshape(-1, D)
            N = x_flat.shape[0]
            logits = x_flat @ router_w
            gate_vals, gate_idx = jax.lax.top_k(logits, TOP_K)
            gate_w = jax.nn.softmax(gate_vals, axis=-1)
            gates = jnp.zeros_like(logits).at[jnp.arange(N)[:, None], gate_idx].set(gate_w)
            h = jax.nn.gelu(jnp.einsum('nd,edf->enf', x_flat, w1) + b1[:, None, :], approximate=False)
            out = jnp.einsum('enf,efd->end', h, w2) + b2[:, None, :]
            res = x_flat[None, :, :] + out
            mu = jnp.mean(res, axis=-1, keepdims=True)
            var = jnp.mean(jnp.square(res - mu), axis=-1, keepdims=True)
            normed = (res - mu) * jax.lax.rsqrt(var + LN_EPS)
            expert_out = normed * gamma[:, None, :] + beta[:, None, :]
            y = jnp.einsum('end,ne->nd', expert_out, gates)
            return y.reshape(B, S, D)
        return _moe(x, router_w, w1, b1, w2, b2, gamma, beta)

    def _L1_xattn_ref(query, key, value, Wq, Wk, Wv):
        import jax, jax.numpy as jnp
        import numpy as np
        EMBED_DIM = 128
        NUM_HEADS = 16
        HEAD_DIM = EMBED_DIM // NUM_HEADS

        def _xavier_uniform(key, out_dim, in_dim):
            limit = jnp.sqrt(6.0 / (in_dim + out_dim)).astype(jnp.float32)
            return jax.random.uniform(key, (out_dim, in_dim), jnp.float32, -limit, limit)
        B, S, _ = query.shape
        H, Dh = (NUM_HEADS, HEAD_DIM)
        q = (query @ Wq.T).reshape(B, S, H, Dh).transpose(0, 2, 1, 3)
        k = (key @ Wk.T).reshape(B, S, H, Dh).transpose(0, 2, 1, 3)
        v = (value @ Wv.T).reshape(B, S, H, Dh).transpose(0, 2, 1, 3)
        scale = 1.0 / jnp.sqrt(jnp.asarray(Dh, q.dtype))
        logits = jnp.einsum('bhqd,bhkd->bhqk', q, k) * scale
        attn = jax.nn.softmax(logits, axis=-1)
        out = jnp.einsum('bhqk,bhkd->bhqd', attn, v)
        out = out.transpose(0, 2, 1, 3).reshape(B, S, H * Dh)
        return out

    def _L1_ffn_ref(x, router_w, router_bias, gate_w, up_w, down_w, sgate_w, sup_w, sdown_w):
        import jax, jax.numpy as jnp
        import numpy as np
        TOPK = 4
        B, T, D = x.shape
        flat = x.reshape(B * T, D)
        logits = flat.astype(jnp.float32) @ router_w.T + router_bias
        scores = jax.nn.softmax(logits, axis=-1)
        topk_scores, topk_idx = jax.lax.top_k(scores, TOPK)
        topk_scores = topk_scores / jnp.clip(topk_scores.sum(axis=-1, keepdims=True), 1e-12, None)
        h = jax.nn.silu(jnp.einsum('nd,ehd->neh', flat, gate_w)) * jnp.einsum('nd,ehd->neh', flat, up_w)
        expert_out = jnp.einsum('neh,edh->ned', h, down_w)
        sel = jnp.take_along_axis(expert_out, topk_idx[:, :, None], axis=1)
        out = (sel * topk_scores.astype(flat.dtype)[:, :, None]).sum(axis=1)
        out = out + jax.nn.silu(flat @ sgate_w.T) * (flat @ sup_w.T) @ sdown_w.T
        return out.reshape(B, T, D)

    def _L2_xattn_ref(q, kv, Wq, Wkv, Wc):
        import jax, jax.numpy as jnp
        import numpy as np
        N_HEAD = 16
        b, l, d = q.shape
        h = N_HEAD
        dh = d // h
        qp = jnp.einsum('bld,ed->ble', q, Wq)
        scores = jnp.einsum('bld,bmd->blm', qp, kv)
        idx = jnp.argmax(scores, axis=-1)
        mem = jnp.take_along_axis(kv, idx[..., None], axis=1)
        mkv = jnp.einsum('bld,ed->ble', mem, Wkv)
        mk, mv = jnp.split(mkv, 2, axis=-1)
        qh = qp.reshape(b, l, h, dh).transpose(0, 2, 1, 3)
        scale = 1.0 / np.sqrt(dh).astype(np.float32)
        logits = jnp.einsum('bhld,bmd->bhlm', qh, mk) * scale
        attn = jax.nn.softmax(logits, axis=-1)
        out = jnp.einsum('bhlm,bmd->bhld', attn, mv)
        out = out.transpose(0, 2, 1, 3).reshape(b, l, d)
        return jnp.einsum('bld,ed->ble', out, Wc)

    def _L2_ffn_ref(hidden_states, q_w, q_b, k_w, k_b, v_w, v_b, o_w, o_b, router_w, router_b, w1, b1, w2, b2):
        import jax, jax.numpy as jnp
        import numpy as np
        import math
        D = 128
        H = 16
        E = 8
        TOPK = 2
        LAT = D // 2
        KPH = LAT // H
        HD = D // H

        def _forward(hs, q_w, q_b, k_w, k_b, v_w, v_b, o_w, o_b, router_w, router_b, w1, b1, w2, b2):
            B, S, _ = hs.shape
            Q = (hs @ q_w + q_b).reshape(B, S, H, HD).transpose(0, 2, 1, 3)
            K = (hs @ k_w + k_b).reshape(B, S, H, KPH).transpose(0, 2, 1, 3)
            V = (hs @ v_w + v_b).reshape(B, S, H, KPH).transpose(0, 2, 1, 3)
            scores = jnp.einsum('bhsk,bhtk->bhst', Q[..., :KPH], K) / math.sqrt(KPH)
            attn = jax.nn.softmax(scores, axis=-1)
            ao = jnp.einsum('bhst,bhtv->bhsv', attn, V)
            ao = ao.transpose(0, 2, 1, 3).reshape(B, S, H * KPH)
            ao = jnp.concatenate([ao, jnp.zeros((B, S, D - LAT), ao.dtype)], axis=-1)
            mla_out = ao @ o_w + o_b
            probs = jax.nn.softmax(mla_out @ router_w + router_b, axis=-1)
            topw, topi = jax.lax.top_k(probs, TOPK)
            topw = topw / (topw.sum(-1, keepdims=True) + 1e-08)
            combine = jnp.sum(jax.nn.one_hot(topi, E, dtype=probs.dtype) * topw[..., None], axis=-2)
            h1 = jnp.einsum('bsd,edf->ebsf', mla_out, w1) + b1[:, None, None, :]
            h1 = jax.nn.gelu(h1, approximate=False)
            h2 = jnp.einsum('ebsf,efd->ebsd', h1, w2) + b2[:, None, None, :]
            moe_out = jnp.einsum('bse,ebsd->bsd', combine, h2)
            return hs + 0.3 * moe_out
        return _forward(hidden_states, q_w, q_b, k_w, k_b, v_w, v_b, o_w, o_b, router_w, router_b, w1, b1, w2, b2)

    def _L3_xattn_ref(q, v, Wq, bq, Wk, bk, Wv, bv):
        import jax, jax.numpy as jnp
        import numpy as np
        EMBED_DIM = 128
        NUM_HEADS = 16
        B, SQ, SK = (4, 256, 256)
        H = NUM_HEADS
        d = EMBED_DIM // H
        b, sq, _ = q.shape
        sk = v.shape[1]
        qp = q @ Wq + bq
        kp = v @ Wk + bk
        vp = v @ Wv + bv
        qh = qp.reshape(b, sq, H, d)
        kh = kp.reshape(b, sk, H, d)
        vh = vp.reshape(b, sk, H, d)
        scores = jnp.einsum('bqhd,bkhd->bhqk', qh, kh) / np.sqrt(EMBED_DIM)
        att = jax.nn.softmax(scores, axis=-1)
        out = jnp.einsum('bhqk,bkhd->bqhd', att, vh)
        return out.reshape(b, sq, EMBED_DIM)

    def _L3_ffn_ref(x, gate_w, lb_bias, w1, w2, cfc, cproj):
        import jax, jax.numpy as jnp
        import numpy as np
        E = 8
        K = 2
        D = 128
        H = 128
        B, T = (2, 128)
        Bx, Tx, Dx = x.shape
        logits = jnp.einsum('btd,ed->bte', x, gate_w)
        _, idx = jax.lax.top_k(logits + lb_bias, K)
        sel_logits = jnp.take_along_axis(logits, idx, axis=-1)
        w = jax.nn.sigmoid(sel_logits)
        w = w / (jnp.sum(w, axis=-1, keepdims=True) + 1e-06)
        xf = x.reshape(-1, Dx)
        idxf = idx.reshape(-1, K)
        wf = w.reshape(-1, K)
        onehot = jax.nn.one_hot(idxf, E, dtype=wf.dtype)
        we = jnp.einsum('nke,nk->ne', onehot, wf)
        hidden = jnp.square(jax.nn.relu(jnp.einsum('nd,ehd->neh', xf, w1)))
        expert_out = jnp.einsum('neh,edh->ned', hidden, w2)
        moe_out = jnp.einsum('ned,ne->nd', expert_out, we).reshape(Bx, Tx, Dx)
        sh = jnp.square(jax.nn.relu(jnp.einsum('btd,hd->bth', x, cfc)))
        shared = jnp.einsum('bth,dh->btd', sh, cproj)
        return moe_out + shared
    x = x + jnp.tanh(g_xattn[0]) * _L0_xattn_ref(_layernorm(x, axis=-1), ctx_1024, ctx_1024, L0_xattn_igate_kernel, L0_xattn_igate_bias, L0_xattn_fgate_kernel, L0_xattn_fgate_bias, L0_xattn_rms_scale)
    x = x + jnp.tanh(g_ffn[0]) * _L0_ffn_ref(_layernorm(x, axis=-1), L0_ffn_router_w, L0_ffn_w1, L0_ffn_b1, L0_ffn_w2, L0_ffn_b2, L0_ffn_gamma, L0_ffn_beta)
    x = x + jnp.tanh(g_xattn[1]) * _L1_xattn_ref(_layernorm(x, axis=-1), ctx_1024, ctx_1024, L1_xattn_Wq, L1_xattn_Wk, L1_xattn_Wv)
    x = x + jnp.tanh(g_ffn[1]) * _L1_ffn_ref(_layernorm(x, axis=-1), L1_ffn_router_w, L1_ffn_router_bias, L1_ffn_gate_w, L1_ffn_up_w, L1_ffn_down_w, L1_ffn_sgate_w, L1_ffn_sup_w, L1_ffn_sdown_w)
    x = x + jnp.tanh(g_xattn[2]) * _L2_xattn_ref(_layernorm(x, axis=-1), ctx_1024, L2_xattn_Wq, L2_xattn_Wkv, L2_xattn_Wc)
    x = x + jnp.tanh(g_ffn[2]) * _L2_ffn_ref(_layernorm(x, axis=-1), L2_ffn_q_w, L2_ffn_q_b, L2_ffn_k_w, L2_ffn_k_b, L2_ffn_v_w, L2_ffn_v_b, L2_ffn_o_w, L2_ffn_o_b, L2_ffn_router_w, L2_ffn_router_b, L2_ffn_w1, L2_ffn_b1, L2_ffn_w2, L2_ffn_b2)
    x = x + jnp.tanh(g_xattn[3]) * _L3_xattn_ref(_layernorm(x, axis=-1), ctx_1024, L3_xattn_Wq, L3_xattn_bq, L3_xattn_Wk, L3_xattn_bk, L3_xattn_Wv, L3_xattn_bv)
    x = x + jnp.tanh(g_ffn[3]) * _L3_ffn_ref(_layernorm(x, axis=-1), L3_ffn_gate_w, L3_ffn_lb_bias, L3_ffn_w1, L3_ffn_w2, L3_ffn_cfc, L3_ffn_cproj)
    return x

_drawn_inputs = setup_inputs


def setup_inputs(seed=0):
    import zlib

    import numpy as np

    out = dict(_drawn_inputs(seed))
    spreads = {'L0_ffn_b1': (0.0, 0.391),
     'L0_ffn_b2': (0.0, 0.1),
     'L0_ffn_gamma': (1.0, 0.2),
     'L0_ffn_beta': (0.0, 0.1),
     'L1_ffn_router_bias': (0.0, 0.1),
     'L2_ffn_q_b': (0.0, 0.8),
     'L2_ffn_k_b': (0.0, 2.0),
     'L2_ffn_v_b': (0.0, 0.8),
     'L2_ffn_o_b': (0.0, 0.684),
     'L2_ffn_router_b': (0.0, 0.1),
     'L2_ffn_b1': (0.0, 0.8),
     'L2_ffn_b2': (0.0, 0.269),
     'L3_xattn_bq': (0.0, 0.8),
     'L3_xattn_bk': (0.0, 2.0),
     'L3_xattn_bv': (0.0, 0.1),
     'L3_ffn_lb_bias': (0.0, 0.8)}
    factors = {'L0_xattn_igate_bias': 64.0,
     'L0_xattn_rms_scale': 2.861,
     'L2_xattn_Wq': 5.535,
     'L2_xattn_Wkv': 3.255,
     'L2_xattn_Wc': 2.977,
     'L2_ffn_q_w': 8.0,
     'L2_ffn_k_w': 8.0,
     'L2_ffn_v_w': 6.895,
     'L2_ffn_o_w': 6.924,
     'L2_ffn_w1': 8.0,
     'L2_ffn_w2': 8.0,
     'L3_ffn_gate_w': 4.322,
     'L3_ffn_w1': 3.965,
     'L3_ffn_w2': 3.668,
     'L3_ffn_cfc': 5.5,
     'L3_ffn_cproj': 4.477}
    for name, (base, spread) in spreads.items():
        noise = np.random.default_rng([zlib.crc32(name.encode()), seed]).standard_normal(out[name].shape)
        drawn = base * np.exp(spread * noise) if base else spread * noise
        out[name] = jnp.asarray(drawn.astype(out[name].dtype))
    for name, factor in factors.items():
        out[name] = (out[name] * factor).astype(out[name].dtype)
    return out
```

```python
from contextlib import ExitStack

import numpy as np

import concourse.bass as bass
from concourse import mybir

F32 = mybir.dt.float32
F16 = mybir.dt.float16
BF16 = mybir.dt.bfloat16
U32 = mybir.dt.uint32
ALU = mybir.AluOpType
ACT = mybir.ActivationFunctionType
X_AXIS = mybir.AxisListType.X

P = 128
B, S, D = 8, 256, 128
N = B * S
T = N // P
CH = 512
NC_ = N // CH
TC = CH // P
BLK = 32
HG = P // BLK
SHIFT = 1024.0
NEG = -1e30
LN_EPS = 1e-5


class Steps:

    def __init__(self, sem):
        self.sem, self.n = sem, 0

    def inc(self, ins):
        ins.then_inc(self.sem, 1)
        self.n = self.n + 1

    def link(self, eng, ins):
        self.inc(ins)
        eng.wait_ge(self.sem, self.n)


class Ctx:
    pass



def layer_norm(nc, k, final_pool=None):
    k.ln_calls += 1
    c0 = k.ln_calls - 1
    with nc.Block() as block:
        @block.vector
        def _(dve):
            st = k.dve_steps
            for t in range(T):
                st.inc(nc.vector.bn_stats(k.stats[:, t, :], k.x[:, t, :]))
            dve.wait_ge(st.sem, st.n)
            for t in range(T):
                st.inc(nc.vector.bn_aggr(k.mv[:, t, :], k.stats[:, t, :]))
            dve.wait_ge(st.sem, st.n)
            nc.vector.tensor_scalar(k.std[:, :], k.mv[:, :, 1], LN_EPS, None, ALU.add).then_inc(k.ln_var, 1)
            dve.wait_ge(k.ln_std, c0 + 1)
            st.link(dve, nc.vector.reciprocal(k.rstd[:, :], k.std[:, :]))
            for t in range(T):
                nc.vector.tensor_scalar(k.xn[:, t, :], k.x[:, t, :], k.mv[:, t, 0:1], k.rstd[:, t:t + 1],
                                        ALU.subtract, ALU.mult).then_inc(k.ln_xn, 1)

        @block.tensor
        def _(pe):
            for t in range(T):
                pe.wait_ge(k.ln_xn, c0 * T + t + 1)
                nc.tensor.transpose(k.ps[:, t // TC, (t % TC) * P:(t % TC + 1) * P], k.xn[:, t, :],
                                    k.ident[:, :]).then_inc(k.ln_tp, 1)

        @block.scalar
        def _(act):
            act.wait_ge(k.ln_var, c0 + 1)
            nc.scalar.activation(k.std[:, :], k.std[:, :], ACT.Sqrt).then_inc(k.ln_std, 1)
            for c in range(NC_):
                act.wait_ge(k.ln_tp, c0 * T + TC * (c + 1))
                nc.scalar.activation(k.xnT[:, c * CH:(c + 1) * CH], k.ps[:, c, :], ACT.Copy)



def setup(nc, k):
    loads = [(k.x[:, :, :], k.d["x"].rearrange("(t p) d -> p t d", p=P)),
             (k.ident[:, :], k.d["ident"]), (k.gates_raw[:, :], k.d["g_all"]),
             (k.attn[:, :, :], k.d["ctx"].rearrange("(t p) d -> p t d", p=P)),
             (k.identh[:, :], k.d["identh"]), (k.consts[:, :], k.d["consts"]),
             (k.misc[:, 0:S + P], k.d["cmask"]), (k.iota[:, :], k.d["iota"]),
             (k.sel32[:, :], k.d["sel32"])]
    loads += [(k.w[n][:], k.d[n]) for n in k.w]
    with nc.Block() as block:
        @block.sync
        def _(sp):
            for dst, src in loads:
                sp.dma_start(dst, src).then_inc(k.setup_in, 16)

        @block.tensor
        def _(pe):
            pe.wait_ge(k.setup_in, 16 * len(loads))
            for t in range(T):
                nc.tensor.transpose(k.ps[:, t // TC, (t % TC) * P:(t % TC + 1) * P], k.attn[:, t, :],
                                    k.ident[:, :]).then_inc(k.ctx_tp, 1)

        @block.scalar
        def _(act):
            act.wait_ge(k.setup_in, 16 * len(loads))
            nc.scalar.activation(k.tanh_g[:, :], k.gates_raw[:, :], ACT.Tanh)
            for c in range(NC_):
                act.wait_ge(k.ctx_tp, TC * (c + 1))
                nc.scalar.activation(k.ctxT[:, c * CH:(c + 1) * CH], k.ps[:, c, :], ACT.Copy)

        @block.gpsimd
        def _(pool):
            nc.gpsimd.memset(k.NM[:, :, :, :], 0.0)

        @block.vector
        def _(dve):
            dve.wait_ge(k.setup_in, 16 * len(loads))
            nc.vector.tensor_copy(k.cmask[:, :], k.misc[:, 0:S + P])
            nc.vector.tensor_copy(k.identb[:, :], k.ident[:, :])



def mlstm(nc, k):
    NH, HD = 4, 32
    R = B * NH
    W3 = S + P
    SC = float(1.0 / np.sqrt(HD))
    wide = k.P4
    g_ = [k.misc[0:R, i * S:(i + 1) * S] for i in range(8)]
    f_, nf, ex, cs, a_, M_, nM, em = g_
    aT, emT = k.small[:, 0:2 * R].rearrange("p (t r) -> p t r", t=2), k.small[:, 64:64 + 2 * R].rearrange("p (t r) -> p t r", t=2)
    ss = k.small[:, 128:128 + T * NH]
    Vm = k.V[:, 0:T * NH * (HD + 1)].rearrange("p (t h e) -> p t h e", t=T, h=NH)
    wg = k.w["l0_gate"][:, :].rearrange("p (c n) -> p c n", c=3)
    gb = k.w["l0_gbias"]
    dT = [wide[:, i * W3:(i + 1) * W3] for i in range(2)]
    cT = [wide[:, (2 + i) * W3:(3 + i) * W3] for i in range(2)]
    nrm = wide[:, 4 * W3:4 * W3 + 64]
    rms = wide[:, 4 * W3 + 64:4 * W3 + 192]
    sq = wide[:, 4 * W3 + 192:4 * W3 + 448]
    s_w, s_g, s_ps, s_f, s_tp, s_st, s_L, s_d, s_c, s_o, s_nrm, s_v, s_var, s_std = [
        k.sem("l0_" + n) for n in ("gate_w", "gate_mm", "gate_act", "gate_dve", "gate_tp", "scores", "logdecay",
                                   "decay", "weighted", "out", "normed", "values", "var", "std")]
    s_tt = k.sem("l0_gate_cols")

    def normalise(dve, st, b):
        o = k.ps[:, 4 + b % 2, 0:2 * NH * (HD + 1)].rearrange("p (t h e) -> p t h e", t=2, h=NH)
        n = nrm[:, 0:2 * NH].rearrange("p (t h) -> p t h", t=2)
        dve.wait_ge(s_o, NH * (b + 1))
        st.link(dve, nc.vector.tensor_tensor(n, o[:, :, :, HD], emT[:, :, NH * b:NH * b + NH], ALU.max))
        st.link(dve, nc.vector.tensor_scalar(n, n, 1e-6, None, ALU.add))
        st.link(dve, nc.vector.reciprocal(n, n))
        at = k.attn[:, 2 * b:2 * b + 2, :].rearrange("p t (h e) -> p t h e", h=NH)
        ins = nc.vector.tensor_tensor(at, o[:, :, :, 0:HD], n.unsqueeze(3).to_broadcast([P, 2, NH, HD]), ALU.mult)
        ins.then_inc(s_nrm, 1)
        dve.wait_ge(s_nrm, b + 1)
        st.link(dve, nc.vector.tensor_tensor(sq.rearrange("p (t e) -> p t e", t=2), k.attn[:, 2 * b:2 * b + 2, :],
                                             k.attn[:, 2 * b:2 * b + 2, :], ALU.mult))
        st.link(dve, nc.vector.tensor_reduce(ss[:, 2 * NH * b:2 * NH * (b + 1)],
                                             sq.rearrange("p (g e) -> p g e", e=HD), X_AXIS, ALU.add))

    with nc.Block() as block:
        @block.sync
        def _(sp):
            for t in range(T):
                sp.dma_start(Vm[:, t, :, 0:HD], k.d["ctx"][t * P:(t + 1) * P, :].rearrange("p (h e) -> p h e", h=NH)
                             ).then_inc(s_v, 16)

        @block.gpsimd
        def _(pool):
            nc.gpsimd.memset(Vm[:, :, :, HD:HD + 1], 1.0).then_inc(s_v, 1)

        @block.tensor
        def _(pe):
            pe.wait_ge(s_w, 1)
            out = k.ps[0:2 * R, 6, 0:S]
            for b in range(B):
                w0 = NH * (B - 1 - b)
                for c, src in ((0, k.xnT), (1, k.ctxT)):
                    mm = nc.tensor.matmul(out, wg[:, c, w0:w0 + 2 * R], src[:, b * S:(b + 1) * S],
                                          start=(b == 0 and c == 0), stop=(b == B - 1 and c == 1))
            mm.then_inc(s_g, 1)
            pe.wait_ge(s_f, 2)
            for i, src in enumerate((a_, em)):
                for t in range(2):
                    mm = nc.tensor.transpose(k.ps[:, 7, 64 * i + 32 * t:64 * i + 32 * t + 32],
                                             src[:, t * P:(t + 1) * P], k.ident[0:R, 0:R])
            mm.then_inc(s_tp, 1)

            def scores(r):
                b, h = divmod(r, NH)
                hs = slice(HD * h, HD * h + HD)
                if r >= 2:
                    pe.wait_ge(s_c, r - 1)
                st, lg = k.ps[:, r % 2, :], k.ps[:, 2 + r % 2, :]
                nc.tensor.matmul(st[:, 0:S], k.ctxT[hs, b * S:b * S + P], k.xnT[hs, b * S:(b + 1) * S], start=True, stop=True)
                nc.tensor.matmul(st[:, S:W3], k.ctxT[hs, b * S + P:(b + 1) * S], k.xnT[hs, b * S + P:(b + 1) * S],
                                 start=True, stop=True).then_inc(s_st, 1)
                if r >= 2:
                    pe.wait_ge(s_d, r - 1)
                nc.tensor.matmul(lg[:, 0:W3], k.identb[:, :], k.cmask[:, :], start=True, stop=False, skip_group_check=True)
                sel = k.sel32[:, r * P:(r + 1) * P]
                nc.tensor.matmul(lg[:, 0:S], sel, nM[:, :], start=False, stop=False, skip_group_check=True)
                nc.tensor.matmul(lg[:, S:W3], sel, nM[:, P:S], start=False, stop=True,
                                 skip_group_check=True).then_inc(s_L, 1)

            def weigh(r):
                b, h = divmod(r, NH)
                pe.wait_ge(s_c, r + 1)
                if h == 0 and b >= 2:
                    pe.wait_ge(s_nrm, b - 1)
                o = k.ps[:, 4 + b % 2, 0:2 * NH * (HD + 1)].rearrange("p (t h e) -> p t h e", t=2, h=NH)
                c = cT[r % 2]
                nc.tensor.matmul(o[:, 0, h, :], c[:, 0:P], Vm[:, 2 * b, h, :], start=True, stop=True)
                nc.tensor.matmul(o[:, 1, h, :], c[:, P:S], Vm[:, 2 * b, h, :], start=True, stop=False)
                nc.tensor.matmul(o[:, 1, h, :], c[:, S:W3], Vm[:, 2 * b + 1, h, :], start=False, stop=True).then_inc(s_o, 1)

            pe.wait_ge(s_f, 3)
            pe.wait_ge(s_v, 16 * T + 1)
            for r in range(R + 1):
                if r < R:
                    scores(r)
                if r:
                    weigh(r - 1)

        @block.scalar
        def _(act):
            st = k.act_steps
            act.wait_ge(s_g, 1)
            st.link(act, nc.scalar.activation(f_[:, :], k.ps[R:2 * R, 6, 0:S], ACT.Identity, bias=gb[0:R, 1:2]))
            nc.scalar.activation(nf[:, :], f_[:, :], ACT.Abs).then_inc(s_ps, 1)
            act.wait_ge(s_ps, 1)
            st.link(act, nc.scalar.activation(ex[:, :], nf[:, :], ACT.Exp, scale=-1.0))
            nc.scalar.activation(cs[:, :], ex[:, :], ACT.Ln, bias=1.0).then_inc(s_ps, 1)
            act.wait_ge(s_f, 1)
            nc.scalar.activation(em[:, :], M_[:, :], ACT.Exp, scale=-1.0).then_inc(s_f, 1)
            act.wait_ge(s_tt, 1)
            for r in range(R):
                act.wait_ge(s_L, r + 1)
                if r >= 2:
                    act.wait_ge(s_c, r - 1)
                lg = k.ps[:, 2 + r % 2, :]
                nc.scalar.activation(dT[r % 2][:, 0:S], lg[:, 0:S], ACT.Exp, bias=aT[:, 0, r:r + 1])
                nc.scalar.activation(dT[r % 2][:, S:W3], lg[:, S:W3], ACT.Exp, bias=aT[:, 1, r:r + 1]).then_inc(s_d, 1)
            act.wait_ge(s_var, 1)
            nc.scalar.activation(ss, ss, ACT.Sqrt).then_inc(s_std, 1)

        @block.vector
        def _(dve):
            st = k.dve_steps
            nc.vector.tensor_tensor(wg[:, 1], wg[:, 1], wg[:, 2], ALU.add).then_inc(s_w, 1)
            st.link(dve, nc.vector.memset(k.zeros[0:R, 0:S], 0.0))
            dve.wait_ge(s_ps, 2)
            st.link(dve, nc.vector.scalar_tensor_tensor(ex[:, :], f_[:, :], 0.0, cs[:, :], ALU.min, ALU.subtract))
            st.link(dve, nc.vector.tensor_tensor_scan(cs[:, :], ex[:, :], k.zeros[0:R, 0:S], 0.0, ALU.add, ALU.add))
            st.link(dve, nc.vector.scalar_tensor_tensor(a_[:, :], k.ps[0:R, 6, 0:S], gb[0:R, 0:1], cs[:, :], ALU.add, ALU.subtract))
            st.link(dve, nc.vector.tensor_tensor_scan(nf[:, :], a_[:, :], a_[:, :], -3e38, ALU.max, ALU.max))
            nc.vector.tensor_tensor(M_[:, :], cs[:, :], nf[:, :], ALU.add).then_inc(s_f, 1)
            dve.wait_ge(s_f, 2)
            nc.vector.tensor_scalar(nM[:, :], nf[:, :], -1.0, None, ALU.mult).then_inc(s_f, 1)
            dve.wait_ge(s_tp, 1)
            nc.vector.tensor_copy(k.small[:, 0:128], k.ps[:, 7, 0:128]).then_inc(s_tt, 1)
            for r in range(R):
                b, h = divmod(r, NH)
                dve.wait_ge(s_st, r + 1)
                dve.wait_ge(s_d, r + 1)
                if r >= 2:
                    dve.wait_ge(s_o, r - 1)
                nc.vector.scalar_tensor_tensor(cT[r % 2][:, :], k.ps[:, r % 2, 0:W3], SC, dT[r % 2][:, :],
                                               ALU.mult, ALU.mult).then_inc(s_c, 1)
                if h == 0 and b:
                    normalise(dve, st, b - 1)
            normalise(dve, st, B - 1)
            st.link(dve, nc.vector.tensor_scalar(ss, ss, 1.0 / HD, 1e-6, ALU.mult, ALU.add))
            nc.vector.tensor_scalar(rms, k.w["l0_rms"][:, :], 1.0, None, ALU.add).then_inc(s_var, 1)
            dve.wait_ge(s_std, 1)
            st.link(dve, nc.vector.reciprocal(ss, ss))
            at = k.attn[:, :, :].rearrange("p t (h e) -> p t h e", h=NH)
            st.link(dve, nc.vector.tensor_tensor(at, at, ss.rearrange("p (t h) -> p t h", h=NH).unsqueeze(3).to_broadcast([P, T, NH, HD]), ALU.mult))
            st.link(dve, nc.vector.tensor_tensor(k.attn[:, :, :], k.attn[:, :, :], rms.unsqueeze(1).to_broadcast([P, T, D]), ALU.mult))
            st.link(dve, nc.vector.scalar_tensor_tensor(k.x[:, :, :], k.attn[:, :, :], k.tanh_g[:, 0:1], k.x[:, :, :], ALU.mult, ALU.add))



def aux_views(k, spec):
    out, at = {}, 0
    for name, width in spec:
        out[name] = k.aux[:, at:at + width]
        at += width
    return out


def load_layer(nc, k, cfg, sp):
    tag, E, per = cfg["tag"], cfg["E"], cfg["per"]
    width = k.d[tag + "_aux"].shape[1]
    sp.dma_start(k.aux[:, 0:width], k.d[tag + "_aux"]).then_inc(k.aux_in, 16)
    k.aux_n += 1
    k.w_n += 1
    for q in range(4):
        a, b = E * q // 4 * per, E * (q + 1) // 4 * per
        sp.dma_start(k.big[:, a:b], k.d[tag + "_w"][:, a:b]).then_inc(k.w_in[q], 16)


def route(nc, k, cfg):
    tag, E, K = cfg["tag"], cfg["route_E"], cfg["K"]
    kind = cfg["route"]
    src = cfg["src"](k)
    a = aux_views(k, cfg["aux"])
    L = k.misc[:, 0:T * E].rearrange("p (t e) -> p t e", e=E)
    Lb = k.misc[:, 512:512 + T * E].rearrange("p (t e) -> p t e", e=E)
    eq = k.misc[:, 1024:1024 + T * E].rearrange("p (t e) -> p t e", e=E)
    tmp = k.misc[:, 1536:1536 + T * E].rearrange("p (t e) -> p t e", e=E)
    top = k.small[:, 0:8 * T].rearrange("p (t j) -> p t j", j=8)
    idx = k.small[:, 8 * T:16 * T].rearrange("p (t j) -> p t j", j=8)
    w = k.small[:, 16 * T:(16 + K) * T].rearrange("p (t j) -> p t j", j=K)
    one = k.small[:, 24 * T:25 * T]
    idx_i = k.idx_i[:, :].rearrange("p (t j) -> p t j", j=8)
    G = k.G[:, :, 0:E]
    gT = k.V[0:E, 0:N]
    s_mm, s_arg, s_exp, s_g, s_tp, s_ev, s_b = [k.sem(f"{tag}_r_{n}") for n in
                                         ("logits", "exp_arg", "exp", "gates", "gates_tp", "gates_T", "bias")]
    has_bias_rows = "bias_rows" in a
    with nc.Block() as block:
        @block.sync
        def _(sp):
            load_layer(nc, k, cfg, sp)

        @block.tensor
        def _(pe):
            pe.wait_ge(k.aux_in, 16 * k.aux_n)
            for t in range(T):
                mm = nc.tensor.matmul(k.ps[:, 7, t * E:(t + 1) * E], src[:, t * P:(t + 1) * P], a["router"],
                                      start=True, stop=True)
            mm.then_inc(s_mm, 1)
            if has_bias_rows:
                pe.wait_ge(s_g, 1)
                for t in range(T):
                    mm = nc.tensor.transpose(k.ps[0:E, t // TC, (t % TC) * P:(t % TC + 1) * P], G[:, t, :], k.ident[:, :])
                mm.then_inc(s_tp, 1)
                pe.wait_ge(s_ev, 1)
                for t in range(T):
                    mm = nc.tensor.matmul(k.ps[:, t // TC, (t % TC) * P:(t % TC + 1) * P], gT[:, t * P:(t + 1) * P],
                                          a["bias_rows"][0:E, :], start=True, stop=True)
                mm.then_inc(s_b, 1)

        @block.scalar
        def _(act):
            act.wait_ge(s_arg, 1)
            nc.scalar.activation(w, w, ACT.Exp, scale=-1.0 if kind == "sigmoid" else 1.0).then_inc(s_exp, 1)
            if kind == "softmax_all":
                nc.scalar.activation(eq, eq, ACT.Exp).then_inc(s_exp, 1)
            if has_bias_rows:
                act.wait_ge(s_tp, 1)
                nc.scalar.activation(gT, k.ps[0:E, 0:4, :].rearrange("p a b -> p (a b)"), ACT.Copy).then_inc(s_ev, 1)
                act.wait_ge(s_b, 1)
                nc.scalar.activation(k.attn[:, :, :], k.ps[:, 0:4, :].rearrange("p a (t d) -> p (a t) d", d=D), ACT.Copy)

        @block.vector
        def _(dve):
            st = k.dve_steps
            dve.wait_ge(s_mm, 1)
            ps = k.ps[:, 7, 0:T * E].rearrange("p (t e) -> p t e", e=E)
            def bias():
                return a["router_bias"].unsqueeze(1).to_broadcast([P, T, E])
            if kind == "softmax_all":
                st.link(dve, nc.vector.tensor_tensor(L, ps, bias(), ALU.add))
            else:
                st.link(dve, nc.vector.tensor_copy(L, ps))
            pick = L
            if kind == "sigmoid":
                st.link(dve, nc.vector.tensor_tensor(Lb, L, bias(), ALU.add))
                pick = Lb
            for t in range(T):
                st.inc(nc.vector.max(top[:, t, :], pick[:, t, :]))
            dve.wait_ge(st.sem, st.n)
            for t in range(T):
                st.inc(nc.vector.max_index(idx_i[:, t, :], top[:, t, :], pick[:, t, :]))
            dve.wait_ge(st.sem, st.n)
            st.link(dve, nc.vector.tensor_copy(idx, idx_i))

            def onehot(j):
                st.link(dve, nc.vector.tensor_tensor(eq, k.iota[:, 0:E].unsqueeze(1).to_broadcast([P, T, E]),
                                                     idx[:, :, j:j + 1].to_broadcast([P, T, E]), ALU.is_equal))
            if kind == "sigmoid":
                for j in range(K):
                    onehot(j)
                    st.link(dve, nc.vector.tensor_tensor(tmp, eq, L, ALU.mult))
                    st.link(dve, nc.vector.tensor_reduce(w[:, :, j:j + 1].rearrange("p t j -> p (t j)"), tmp, X_AXIS, ALU.add))
                nc.vector.memset(one, 0.0).then_inc(s_arg, 1)
                dve.wait_ge(s_exp, 1)
                st.link(dve, nc.vector.tensor_scalar(w, w, 1.0, None, ALU.add))
                st.link(dve, nc.vector.reciprocal(w, w))
                guard, floor = ALU.add, 1e-6
            else:
                if kind == "softmax_all":
                    st.link(dve, nc.vector.tensor_tensor(eq, L, top[:, :, 0:1].to_broadcast([P, T, E]), ALU.subtract))
                nc.vector.tensor_tensor(w, top[:, :, 0:K], top[:, :, 0:1].to_broadcast([P, T, K]), ALU.subtract).then_inc(s_arg, 1)
                guard, floor = None, None
                dve.wait_ge(s_exp, 1)
                if kind == "softmax_all":
                    dve.wait_ge(s_exp, 2)
                    st.link(dve, nc.vector.tensor_reduce(one, eq, X_AXIS, ALU.add))
                    st.link(dve, nc.vector.reciprocal(one, one))
                    st.link(dve, nc.vector.tensor_tensor(w, w, one.unsqueeze(2).to_broadcast([P, T, K]), ALU.mult))
                    guard, floor = cfg["guard"]
            st.link(dve, nc.vector.tensor_reduce(one, w, X_AXIS, ALU.add))
            if guard is not None:
                st.link(dve, nc.vector.tensor_scalar(one, one, floor, None, guard))
            st.link(dve, nc.vector.reciprocal(one, one))
            st.link(dve, nc.vector.tensor_tensor(w, w, one.unsqueeze(2).to_broadcast([P, T, K]), ALU.mult))
            if cfg["E"] > E:
                st.inc(nc.vector.memset(k.G[:, :, E:cfg["E"]], 1.0))
            for j in range(K):
                onehot(j)
                wj = w[:, :, j:j + 1].to_broadcast([P, T, E])
                if j == 0:
                    ins = nc.vector.tensor_tensor(G, eq, wj, ALU.mult)
                else:
                    st.link(dve, nc.vector.tensor_tensor(tmp, eq, wj, ALU.mult))
                    ins = nc.vector.tensor_tensor(G, G, tmp, ALU.add)
                if j < K - 1:
                    st.link(dve, ins)
            ins.then_inc(s_g, 1)


def moe(nc, k, cfg):
    tag, E, nf, per, kind = cfg["tag"], cfg["E"], cfg["nf"], cfg["per"], cfg["kind"]
    nub = 2 if kind == "swiglu" else nf
    R = 2 if E % 2 == 0 else 3
    nU = 4 if R == 2 else 3
    src = cfg["src"](k)
    a = aux_views(k, cfg["aux"])
    gate_col = cfg["gate_col"]
    H = [k.P4[:, i * nf * CH:(i + 1) * nf * CH].rearrange("p (f n) -> p f n", f=nf) for i in range(R)]
    SG = [k.P4[:, (R + i) * CH:(R + i + 1) * CH] for i in range(R)] if kind in ("swiglu", "relu2") else None
    acc = k.acc[:, :].rearrange("p (t d) -> p t d", t=TC)
    Rs = [k.misc[:, i * CH:(i + 1) * CH].rearrange("p (t d) -> p t d", t=TC) for i in range(2)]
    xb = [k.misc[:, (2 + i) * CH:(3 + i) * CH].rearrange("p (t d) -> p t d", t=TC) for i in range(2)]
    fst = [k.small[:, 32 * i:32 * i + 24].rearrange("p (t s) -> p t s", t=TC) for i in range(2)]
    fmv = [k.small[:, 64 + 8 * i:72 + 8 * i].rearrange("p (t s) -> p t s", t=TC) for i in range(2)]
    fvar = [k.small[:, 80 + 4 * i:84 + 4 * i] for i in range(2)]
    frs = [k.small[:, 88 + 4 * i:92 + 4 * i] for i in range(2)]
    fw = [k.small[:, 96 + 4 * i:100 + 4 * i] for i in range(2)]
    mhalf = k.small[:, 104:108]
    s_up, s_act, s_h, s_dn, s_cb, s_xb, s_R, s_var, s_rs, s_ch, s_ser = [k.sem(f"{tag}_{n}") for n in
        ("up", "act", "hidden", "down", "combined", "residual", "summed", "var", "rstd", "chunk", "serial")]

    def wt(e, i):
        return k.big[:, e * per + i * P:e * per + (i + 1) * P]

    def chunks(eng, body):
        body(0)
        with eng.Fori(1, NC_) as c:
            body(c)

    first = lambda c: isinstance(c, int)

    with nc.Block() as block:
        @block.tensor
        def _(pe):
            def chunk(c):
                for e in range(E + 1):
                    if e < E:
                        if first(c) and any(e == E * q // 4 for q in range(4)):
                            pe.wait_ge(k.w_in[[E * q // 4 for q in range(4)].index(e)], 16 * k.w_n)
                        for f in range(nub):
                            i = e * nub + f
                            if not (first(c) and i < nU):
                                if kind == "swiglu":
                                    pe.wait_ge((s_act, s_h)[f], c * E + e - 1)
                                elif kind == "relu2":
                                    pe.wait_ge(s_act, c * E + e - 2)
                                else:
                                    pe.wait_ge(s_act, c * (E * nub) + i - nU + 1)
                            nc.tensor.matmul(k.ps[:, i % nU, :], wt(e, f), src[:, bass.ds(c * CH, CH)],
                                             start=True, stop=True).then_inc(s_up, 1)
                    if e:
                        o, hb = (e - 1) % R, H[(e - 1) % R]
                        if kind in ("swiglu", "relu2"):
                            pe.wait_ge(s_h, c * E + e)
                        else:
                            pe.wait_ge(s_act, c * (E * nub) + e * nub)
                        if not (first(c) and e - 1 < R):
                            pe.wait_ge(s_cb, c * E + e - R)
                        for tt in range(TC):
                            for f in range(nf):
                                mm = nc.tensor.matmul(k.ps[:, 4 + o, tt * P:(tt + 1) * P], hb[:, f, tt * P:(tt + 1) * P],
                                                      wt(e - 1, nub + f), start=(f == 0), stop=(f == nf - 1))
                        mm.then_inc(s_dn, 1)
            chunks(pe, chunk)

        @block.scalar
        def _(act):
            def chunk(c):
                for e in range(E):
                    if kind in ("swiglu", "relu2"):
                        act.wait_ge(s_up, c * (E * nub) + e * nub + 1)
                        if not (first(c) and e < R):
                            act.wait_ge(s_h, c * E + e - R + 1)
                        nc.scalar.activation(SG[e % R], k.ps[:, (e * nub) % nU, :],
                                             ACT.Silu if kind == "swiglu" else ACT.Relu).then_inc(s_act, 1)
                    else:
                        if not (first(c) and e < R):
                            act.wait_ge(s_dn, c * E + e - R + 1)
                        for f in range(nf):
                            i = e * nub + f
                            act.wait_ge(s_up, c * (E * nub) + i + 1)
                            nc.scalar.activation(H[e % R][:, f, :], k.ps[:, i % nU, :], ACT.Gelu,
                                                 bias=a["b1"][:, e * nf + f:e * nf + f + 1]).then_inc(s_act, 1)
            chunks(act, chunk)

        @block.gpsimd
        def _(pool):
            if kind != "gelu_ln":
                return
            nc.gpsimd.memset(mhalf, -0.5).then_inc(s_ser, 1)
            pool.wait_ge(s_ser, 1)

            def chunk(c):
                def residual(e):
                    if not (first(c) and e < 2):
                        pool.wait_ge(s_R, c * E + e - 1)
                        nc.gpsimd.tensor_tensor(k.pjunk[:, e:e + 1], k.consts[:, 0:1], k.consts[:, 0:1], ALU.add)
                    nc.gpsimd.tensor_tensor(xb[e % 2], k.xn[:, bass.ds(c * TC, TC), :],
                                            a["b2"][:, e * D:(e + 1) * D].unsqueeze(1).to_broadcast([P, TC, D]),
                                            ALU.add).then_inc(s_xb, 1)
                residual(0)
                for e in range(E):
                    if e + 1 < E:
                        residual(e + 1)
                    pool.wait_ge(s_var, c * E + e + 1)
                    nc.gpsimd.tensor_tensor(frs[e % 2], fvar[e % 2], mhalf, ALU.pow).then_inc(s_rs, 1)
            chunks(pool, chunk)

        @block.vector
        def _(dve):
            st = Steps(s_ser)
            st.n = 1 if kind == "gelu_ln" else 0
            base = st.n
            size = []

            def chunk(c):
                if not first(c):
                    st.n = c * size[0] + base

                def hidden(e):
                    dve.wait_ge(s_act, c * E + e + 1)
                    if kind == "swiglu":
                        dve.wait_ge(s_up, c * (E * nub) + (e + 1) * nub)
                    if not (first(c) and e < R):
                        dve.wait_ge(s_dn, c * E + e - R + 1)
                    other = k.ps[:, (e * nub + 1) % nU, :] if kind == "swiglu" else SG[e % R]
                    nc.vector.tensor_tensor(H[e % R][:, 0, :], SG[e % R], other, ALU.mult).then_inc(s_h, 1)

                def combine(e):
                    dve.wait_ge(s_dn, c * E + e + 1)
                    if e:
                        dve.wait_ge(s_cb, c * E + e)
                    for tt in range(TC):
                        g = k.G[:, bass.ds(c * TC + tt, 1), gate_col(e)].rearrange("p t e -> p (t e)")
                        o = k.ps[:, 4 + e % R, tt * P:(tt + 1) * P]
                        if e == 0:
                            ins = nc.vector.tensor_scalar(acc[:, tt, :], o, g, None, ALU.mult)
                        else:
                            ins = nc.vector.scalar_tensor_tensor(acc[:, tt, :], o, g, acc[:, tt, :], ALU.mult, ALU.add)
                        if tt < TC - 1:
                            st.inc(ins)
                    ins.then_inc(s_cb, 1)

                def stats(e):
                    dve.wait_ge(s_dn, c * E + e + 1)
                    dve.wait_ge(s_xb, c * E + e + 1)
                    nc.vector.tensor_tensor(Rs[e % 2], k.ps[:, 4 + e % R, :].rearrange("p (t d) -> p t d", t=TC), xb[e % 2],
                                            ALU.add).then_inc(s_R, 1)
                    dve.wait_ge(s_R, c * E + e + 1)
                    for tt in range(TC):
                        ins = nc.vector.bn_stats(fst[e % 2][:, tt, :], Rs[e % 2][:, tt, :])
                    ins.then_inc(s_cb, 1)
                    dve.wait_ge(s_cb, c * E + e + 1)
                    nc.vector.memset(k.junk[:, e:e + 1], 0.0)
                    for tt in range(TC):
                        ins = nc.vector.bn_aggr(fmv[e % 2][:, tt, :], fst[e % 2][:, tt, :])
                    st.link(dve, ins)
                    nc.vector.tensor_scalar(fvar[e % 2], fmv[e % 2][:, :, 1], 1e-6, None, ALU.add).then_inc(s_var, 1)

                def normed(e):
                    dve.wait_ge(s_rs, c * E + e + 1)
                    g = k.G[:, bass.ds(c * TC, TC), gate_col(e)].rearrange("p t e -> p (t e)")
                    st.link(dve, nc.vector.tensor_tensor(fw[e % 2], frs[e % 2], g, ALU.mult))
                    for tt in range(TC):
                        ins = nc.vector.tensor_scalar(Rs[e % 2][:, tt, :], Rs[e % 2][:, tt, :], fmv[e % 2][:, tt, 0:1],
                                                      fw[e % 2][:, tt:tt + 1], ALU.subtract, ALU.mult)
                    st.link(dve, ins)
                    gam = a["gamma"][:, e * D:(e + 1) * D].unsqueeze(1).to_broadcast([P, TC, D])
                    if e == 0:
                        ins = nc.vector.tensor_tensor(acc, Rs[e % 2], gam, ALU.mult)
                    else:
                        st.link(dve, nc.vector.tensor_tensor(Rs[e % 2], Rs[e % 2], gam, ALU.mult))
                        ins = nc.vector.tensor_tensor(acc, acc, Rs[e % 2], ALU.add)
                    st.link(dve, ins)

                for e in range(E + 1):
                    if kind == "gelu_ln":
                        if e < E:
                            stats(e)
                        if e:
                            normed(e - 1)
                    elif kind == "gelu":
                        if e < E:
                            combine(e)
                    else:
                        if e < E:
                            hidden(e)
                        if e:
                            combine(e - 1)
                dve.wait_ge(s_cb, c * E + E)
                tiles = lambda buf: buf[:, bass.ds(c * TC, TC), :]
                if "bias_rows" in a:
                    st.link(dve, nc.vector.tensor_tensor(acc, acc, tiles(k.attn), ALU.add))
                if kind == "gelu":
                    st.link(dve, nc.vector.scalar_tensor_tensor(acc, acc, 0.3, tiles(k.xn), ALU.mult, ALU.add))
                gi = cfg["tanh"]
                st.link(dve, nc.vector.scalar_tensor_tensor(tiles(k.x), acc, k.tanh_g[:, gi:gi + 1], tiles(k.x),
                                                            ALU.mult, ALU.add))
                if first(c):
                    size.append(st.n - base)
            chunks(dve, chunk)


def slot(e):
    return slice(e, e + 1)


CFG0 = dict(tag="l0f", E=8, route_E=8, K=2, nf=4, per=8 * P, kind="gelu_ln", route="softmax_top", tanh=1,
            src=lambda k: k.xnT[:, :], gate_col=slot,
            aux=[("router", 8), ("b1", 32), ("gamma", 8 * D), ("b2", 8 * D), ("bias_rows", D)])
CFG1 = dict(tag="l1f", E=36, route_E=32, K=4, nf=1, per=3 * P, kind="swiglu", route="softmax_all", tanh=3,
            guard=(ALU.max, 1e-12), src=lambda k: k.xnT[:, :], gate_col=slot,
            aux=[("router", 32), ("router_bias", 32)])
CFG2 = dict(tag="l2f", E=8, route_E=8, K=2, nf=2, per=4 * P, kind="gelu", route="softmax_all", tanh=5,
            guard=(ALU.add, 1e-8), src=lambda k: k.xnT[:, :], gate_col=slot,
            aux=[("router", 8), ("router_bias", 8), ("b1", 16), ("bias_rows", D)])
CFG3 = dict(tag="l3f", E=9, route_E=8, K=2, nf=1, per=2 * P, kind="relu2", route="sigmoid", tanh=7,
            src=lambda k: k.xnT[:, :], gate_col=slot,
            aux=[("router", 8), ("router_bias", 8)])


def ffn(cfg):
    def stage(nc, k):
        route(nc, k, cfg)
        moe(nc, k, cfg)
    return stage



NHEAD = 16


class Split:

    def __init__(self, k, tag, n_q, n_all, bias_q, bias_k, sign_q, sign_k, dest):
        self.k, self.n, self.dest = k, n_all, dest
        self.late_ring = 4
        self.q = n_q
        self.bias, self.sign = (bias_q, bias_k), (sign_q, sign_k)
        self.s_mm, self.s_hi, self.s_out = (k.sem(f"{tag}_{n}") for n in ("proj", "split_hi", "split"))
        self.hi = k.hi
        self.v = k.misc

    def side(self, i):
        return 0 if i < self.q else 1

    ring = lambda self, i: self.late_ring if i >= self.q else 4

    def bank(self, i):
        return self.k.ps[:, i % self.ring(i), :]

    def tensor_ready(self, pe, i):
        if i >= 4:
            pe.wait_ge(self.s_out, max(i - self.ring(i) + 1, self.q if self.ring(i) < 4 else 0))

    def scalar(self, nc, act, i):
        act.wait_ge(self.s_mm, i + 1)
        if i >= 2:
            act.wait_ge(self.s_out, i - 1)
        b = self.bias[self.side(i)]
        hi = self.hi[:, i % 2, :]
        if b is None:
            nc.scalar.activation(hi, self.bank(i), ACT.Copy).then_inc(self.s_hi, 1)
        else:
            col = b(i)
            nc.scalar.activation(hi, self.bank(i), ACT.Identity, bias=col)
            nc.scalar.activation(self.v[:, (i % 2) * CH:(i % 2 + 1) * CH], self.bank(i), ACT.Identity,
                                 bias=col).then_inc(self.s_hi, 1)

    def vector(self, nc, dve, i):
        dve.wait_ge(self.s_hi, i + 1)
        b = self.bias[self.side(i)]
        v = self.bank(i) if b is None else self.v[:, (i % 2) * CH:(i % 2 + 1) * CH]
        nc.vector.scalar_tensor_tensor(self.dest(i), self.hi[:, i % 2, :], self.sign[self.side(i)], v, ALU.mult,
                                       ALU.add).then_inc(self.s_out, 1)


def attention(nc, k, cfg):
    tag, kd, dv, scale, mqa = cfg["tag"], cfg["kd"], cfg["dv"], cfg["scale"], cfg["mqa"]
    src_q, src_k = k.xnT, (k.xnT if cfg["self"] else k.ctxT)
    wq = k.w[tag + "_q"]
    wk = k.w[tag + "_k"]
    wv = k.w[tag + "_v"] if tag + "_v" in k.w else None
    bias = k.w.get(tag + "_b")
    bv = k.w.get(tag + "_bv")
    KG = 1 if mqa else 4
    VH = 1 if mqa else NHEAD
    nq, nk = 16, KG * NC_
    V = k.V[:, 0:T * VH * (dv + 1)].rearrange("p (t h e) -> p t h e", t=T, h=VH)
    KZ = k.big[:, :].bitcast(F16).rearrange("p (g j n) -> p g j n", g=4, j=HG)
    Prb = [k.P4[:, i * 1024:(i + 1) * 1024].rearrange("p (j t q) -> p j t q", j=2, t=2) for i in range(4)]
    mx = k.small[:, 0:16].rearrange("p (r t j) -> p r t j", r=2, t=2)
    c0 = 0 if kd == 8 else 2
    order = [(g, c) for g in range(4) for c in range(NC_)]
    qdest = lambda i: k.Qs[:, i // NC_, (i % NC_) * CH:(i % NC_ + 1) * CH]
    kdest = lambda i: k.Kst[:, ((i - nq) // NC_) % 2, ((i - nq) % NC_) * CH:((i - nq) % NC_ + 1) * CH]
    sp_ = Split(k, tag, nq, nq + nk, (lambda i: bias[:, i // NC_:i // NC_ + 1]) if bias is not None else None,
                (lambda i: bias[:, 4 + (i - nq) // NC_:5 + (i - nq) // NC_]) if bias is not None else None,
                k.consts[:, c0:c0 + 1], k.consts[:, c0 + 1:c0 + 2], lambda i: qdest(i) if i < nq else kdest(i))
    s_kz, s_v, s_vc, s_ones = [k.sem(f"{tag}_{n}") for n in ("k_zeroed", "v", "v_copied", "ones")]
    s_place = [k.sem(f"{tag}_k_placed{n}") for n in range(2)]
    sel = cfg.get("select")
    if sel:
        hooks = sel(nc, k, cfg, sp_, V)
    with nc.Block() as block:
        @block.gpsimd
        def _(pool):
            n0 = KG * HG * N // 2
            nc.gpsimd.memset(V[:, :, :, dv:dv + 1], 1.0).then_inc(s_ones, 1)
            nc.gpsimd.memset(k.big[:, 0:n0 // 2], 0.0).then_inc(s_kz, 1)
            pool.wait_ge(s_kz, 2)
            for j in range(HG):
                nc.gpsimd.memset(KZ[BLK * j:BLK * j + 2, 0:KG, j, :], SHIFT).then_inc(s_kz, 1)

        @block.tensor
        def _(pe):
            for i in range(nq):
                g, c = divmod(i, NC_)
                sp_.tensor_ready(pe, i)
                nc.tensor.matmul(sp_.bank(i), wq[:, g * P:(g + 1) * P], src_q[:, c * CH:(c + 1) * CH], start=True,
                                 stop=True).then_inc(sp_.s_mm, 1)
            if sel:
                hooks["pe"](pe)
                return
            for i in range(nq, nq + nk):
                g, c = divmod(i - nq, NC_)
                sp_.tensor_ready(pe, i)
                nc.tensor.matmul(sp_.bank(i), wk[:, g * P:(g + 1) * P], src_k[:, c * CH:(c + 1) * CH], start=True,
                                 stop=True).then_inc(sp_.s_mm, 1)
            nv = VH * dv
            for t in range(T):
                if t % TC == 0 and t >= 3 * TC:
                    pe.wait_ge(s_vc, t // TC - 2)
                o = k.ps[:, 4 + (t // TC) % 3, (t % TC) * P:(t % TC) * P + nv]
                mm = nc.tensor.matmul(o, src_k[:, t * P:(t + 1) * P], wv[:, 0:nv], start=True, stop=bv is None)
                if bv is not None:
                    mm = nc.tensor.matmul(o, k.w["ones"][0:1, :], bv[0:1, 0:nv], start=False, stop=True)
                mm.then_inc(s_v, 1)

        @block.scalar
        def _(act):
            for i in range(nq):
                sp_.scalar(nc, act, i)
            if sel:
                hooks["act"](act)
                return
            for i in range(nq, nq + nk):
                sp_.scalar(nc, act, i)
            act.wait_ge(s_ones, 1)
            for q in range(NC_):
                act.wait_ge(s_v, TC * (q + 1))
                pv = k.ps[:, 4 + q % 3, :].rearrange("p (t n) -> p t n", t=TC)
                for t in range(TC):
                    ins = nc.scalar.activation(V[:, TC * q + t, :, 0:dv], pv[:, t, 0:VH * dv].rearrange("p (h e) -> p h e", h=VH), ACT.Copy)
                ins.then_inc(s_vc, 1)

        @block.vector
        def _(dve):
            n0 = KG * HG * N // 2
            nc.vector.memset(k.big[:, n0 // 2:n0], 0.0).then_inc(s_kz, 1)
            for i in range(nq):
                sp_.vector(nc, dve, i)
            if sel:
                hooks["dve"](dve)
                return
            for i in range(nq, nq + nk):
                if i - nq >= 2 * NC_ and (i - nq) % NC_ == 0:
                    dve.wait_ge(s_place[(i - nq) // NC_ % 2], 16 * HG * ((i - nq) // NC_ // 2))
                sp_.vector(nc, dve, i)

        @block.sync
        def _(sp):
            sp.wait_ge(s_kz, 2 + HG)
            for g in range(KG):
                sp.wait_ge(sp_.s_out, nq + NC_ * (g + 1))
                for j in range(HG):
                    r = slice(BLK * j + 2, BLK * j + BLK)
                    sp.dma_start(KZ[r, g, j, :], k.Kst[r, g % 2, :]).then_inc(s_place[g % 2], 16)
            for g in range(min(KG, 2)):
                sp.wait_ge(s_place[g], 16 * HG * (KG // 2 if KG > 1 else 1))

    s_mx, s_rd, s_hi, s_nm, s_mt, s_qa, s_st, s_ex, s_pv, s_no, s_rc, s_oc, s_oz, s_vg = [k.sem(f"{tag}_{n}") for n in
        ("max_scores", "maxima", "max_hi", "max_parts", "turned", "q_shifted", "scores_T", "probs", "out", "normed",
         "recip", "out_copied", "out_zeroed", "v_staged")]
    MT = k.ps[:, 7, 0:P].bitcast(F16)
    OUTT = k.ps[:, 6, 0:S]
    OT = k.OT
    GH = 1 if mqa else HG
    VG = [k.small[:, 128 + 80 * i:128 + 80 * i + 2 * GH * (dv + 1)].rearrange("p (t j e) -> p t j e", t=2, j=GH) for i in range(2)]
    TP = k.ps[:, 7, S:2 * S].rearrange("p (t j r) -> p t j r", t=2, r=BLK)
    rs = k.small[:, 16:24].rearrange("p (t j) -> p t j", t=2)
    kz_g = (lambda g: 0) if mqa else (lambda g: g)

    def back(b, g, by):
        return (b, g - by) if g >= by else (b - 1, g + 4 - by)

    def live(b):
        return not (isinstance(b, int) and (b < 0 or b >= B))

    def early(b, g, j):
        return isinstance(b, int) and 4 * b + g < j

    def sweep(eng, step):
        for g in range(4):
            step(0, g)
        with eng.Fori(1, B) as b:
            for g in range(4):
                step(b, g)
        for g in range(3):
            step(B, g)

    with nc.Block() as block:
        @block.gpsimd
        def _(pool):
            def step(b, g):
                if not live(b):
                    return
                if not early(b, g, 2):
                    pool.wait_ge(s_pv, 8 * b + 2 * g - 2)
                    nc.gpsimd.tensor_tensor(k.pjunk[:, g:g + 1], k.consts[:, 0:1], k.consts[:, 0:1], ALU.add)
                nc.gpsimd.tensor_copy(VG[g % 2], V[:, bass.ds(2 * b, 2), 0:1 if mqa else NHEAD, :][:, :, 0 if mqa else 4 * g:1 if mqa else 4 * g + 4, :]
                                      ).then_inc(s_vg, 1)
            sweep(pool, step)

        @block.tensor
        def _(pe):
            def max_scores(b, g, js):
                for j in js:
                    if not (early(b, g, 1) and j < 2):
                        pe.wait_ge(s_rd, 16 * b + 4 * g + j - 1)
                    for t in range(2):
                        mm = nc.tensor.matmul(k.ps[:, j % 2, t * S:(t + 1) * S], k.Qs[:, g, bass.ds(b * S + t * P, P)],
                                              KZ[:, kz_g(g), j, bass.ds(b * S, S)], start=True, stop=True)
                    mm.then_inc(s_mx, 1)

            def turn(b, g):
                b1, g1 = back(b, g, 1)
                b3, g3 = back(b, g, 3)
                if live(b1):
                    pe.wait_ge(s_nm, 4 * b1 + g1 + 1)
                    if not early(b1, g1, 1):
                        pe.wait_ge(s_qa, 4 * b1 + g1)
                if live(b3):
                    pe.wait_ge(s_oc, 4 * b3 + g3 + 1)
                    if not early(b3, g3, 1):
                        pe.wait_ge(s_no, 4 * b3 + g3)
                if live(b1):
                    for t in range(2):
                        mm = nc.tensor.transpose(MT[:, t * P:(t + 1) * P], k.NM[:, g1 % 2, t, :], k.identh[:, :])
                if live(b3):
                    for t in range(2):
                        mm = nc.tensor.transpose(k.ps[:, 7, S + t * P:S + (t + 1) * P], OT[:, g3 % 2, t * P:(t + 1) * P],
                                                 k.ident[:, :])
                if live(b1) or live(b3):
                    mm.then_inc(s_mt, 1)

            def scores_T(b, g, hc):
                if hc == 0:
                    pe.wait_ge(s_qa, 4 * b + g + 1)
                if not (early(b, g, 1)):
                    pe.wait_ge(s_ex, 8 * b + 2 * g + hc - 1)
                for jj in range(2):
                    for t in range(2):
                        mm = nc.tensor.matmul(k.ps[:, 2 + 2 * hc + jj, t * S:(t + 1) * S],
                                              KZ[:, kz_g(g), 2 * hc + jj, bass.ds(b * S + t * P, P)], k.Qaug[:, g % 2, :],
                                              start=True, stop=True)
                mm.then_inc(s_st, 1)

            def weigh(b, g, hc):
                pe.wait_ge(s_ex, 8 * b + 2 * g + hc + 1)
                if hc == 0:
                    if early(b, g, 1):
                        pe.wait_ge(s_oz, 1)
                    else:
                        pe.wait_ge(s_oc, 4 * b + g)
                    pe.wait_ge(s_vg, 4 * b + g + 1)
                pr = Prb[(2 * g + hc) % 4]
                for t in range(2):
                    for jj in range(2):
                        j = 2 * hc + jj
                        mm = nc.tensor.matmul(OUTT[BLK * j:BLK * j + dv + 1, :],
                                              VG[g % 2][:, t, 0 if mqa else j, :],
                                              pr[:, jj, t, :], start=(t == 0), stop=(t == 1), skip_group_check=True)
                mm.then_inc(s_pv, 1)

            def step(b, g):
                b1, g1 = back(b, g, 1)
                b2, g2 = back(b, g, 2)
                if live(b):
                    max_scores(b, g, (0, 1))
                turn(b, g)
                if live(b2):
                    weigh(b2, g2, 0)
                if live(b):
                    max_scores(b, g, (2, 3))
                if live(b1):
                    scores_T(b1, g1, 0)
                if live(b2):
                    weigh(b2, g2, 1)
                if live(b1):
                    scores_T(b1, g1, 1)
            sweep(pe, step)

        @block.scalar
        def _(act):
            def step(b, g):
                b1, g1 = back(b, g, 1)
                b2, g2 = back(b, g, 2)
                for hc in range(2):
                    if hc and live(b2):
                        act.wait_ge(s_pv, 8 * b2 + 2 * g2 + 2)
                        if not early(b2, g2, 2):
                            act.wait_ge(s_mt, 4 * b2 + g2 + 1)
                        nc.scalar.activation(OT[:, g2 % 2, :], OUTT, ACT.Copy).then_inc(s_oc, 1)
                    if not live(b1):
                        continue
                    act.wait_ge(s_st, 8 * b1 + 2 * g1 + hc + 1)
                    if not early(b1, g1, 2):
                        act.wait_ge(s_pv, 8 * b1 + 2 * g1 + hc - 3)
                    nc.scalar.activation(Prb[(2 * g1 + hc) % 4].rearrange("p j t q -> p (j t q)"),
                                         k.ps[:, 2 + 2 * hc:4 + 2 * hc, :].rearrange("p a b -> p (a b)"),
                                         ACT.Exp, scale=scale).then_inc(s_ex, 1)
            sweep(act, step)

        @block.vector
        def _(dve):
            def reduce(b, g, js):
                for j in js:
                    dve.wait_ge(s_mx, 16 * b + 4 * g + j + 1)
                    nc.vector.tensor_reduce(mx[:, g % 2, :, j], k.ps[:, j % 2, :].rearrange("p (t n) -> p t n", t=2),
                                            X_AXIS, ALU.max).then_inc(s_rd, 1)

            def parts(b, g):
                nm = k.NM[:, g % 2, :, :].rearrange("p t (j r) -> p t j r", r=BLK)
                dve.wait_ge(s_rd, 16 * b + 4 * g + 4)
                if not early(b, g, 2):
                    dve.wait_ge(s_mt, 4 * b + g - 1)
                nc.vector.tensor_scalar(nm[:, :, :, 0], mx[:, g % 2, :, :], -1.0 / SHIFT, None, ALU.mult).then_inc(s_hi, 1)
                dve.wait_ge(s_hi, 4 * b + g + 1)
                nc.vector.scalar_tensor_tensor(nm[:, :, :, 1], mx[:, g % 2, :, :], -1.0 / SHIFT, nm[:, :, :, 0],
                                               ALU.mult, ALU.subtract).then_inc(s_nm, 1)

            def shift_q(b, g):
                dve.wait_ge(s_mt, 4 * b + g + 1)
                if not early(b, g, 2):
                    dve.wait_ge(s_st, 8 * b + 2 * g - 2)
                nc.vector.tensor_tensor(k.Qaug[:, g % 2, :], MT, k.Qs[:, g, bass.ds(b * S, S)], ALU.add).then_inc(s_qa, 1)

            def normalise(b, g):
                dve.wait_ge(s_mt, 4 * b + g + 3)
                if not early(b, g, 1):
                    dve.wait_ge(s_no, 4 * b + g)
                nc.vector.reciprocal(rs, TP[:, :, :, dv]).then_inc(s_rc, 1)
                dve.wait_ge(s_rc, 4 * b + g + 1)
                at = k.attn[:, bass.ds(2 * b, 2), 4 * g * dv:4 * (g + 1) * dv].rearrange("p t (j e) -> p t j e", j=HG)
                nc.vector.tensor_tensor(at, TP[:, :, :, 0:dv], rs.unsqueeze(3).to_broadcast([P, 2, HG, dv]),
                                        ALU.mult).then_inc(s_no, 1)

            nc.vector.memset(OUTT, 0.0).then_inc(s_oz, 1)

            def step(b, g):
                b1, g1 = back(b, g, 1)
                b3, g3 = back(b, g, 3)
                if live(b):
                    reduce(b, g, (0, 1))
                if live(b1):
                    shift_q(b1, g1)
                if live(b3):
                    normalise(b3, g3)
                if live(b):
                    reduce(b, g, (2, 3))
                    parts(b, g)
            sweep(dve, step)
            if cfg.get("add") is not None:
                gi = cfg["add"]
                dve.wait_ge(s_no, 4 * B)
                nc.vector.scalar_tensor_tensor(k.x[:, :, :], k.attn[:, :, :], k.tanh_g[:, gi:gi + 1], k.x[:, :, :],
                                               ALU.mult, ALU.add)
    if cfg.get("finish"):
        cfg["finish"](nc, k, cfg)


def select_kv(nc, k, cfg, split, V):
    tag, KW = cfg["tag"], P + 8
    qpT = k.attn[:, :, :].rearrange("p t d -> p (t d)")
    kv = k.P4[:, 0:T * KW].rearrange("p (t n) -> p t n", n=KW)
    OHT = [k.P4[:, T * KW + i * 2 * S:T * KW + (i + 1) * 2 * S].rearrange("p (m l) -> p m l", m=2) for i in range(2)]
    OH = [k.misc[:, i * S:(i + 1) * S] for i in range(4)]
    top, idx = k.small[:, 64:72], k.small[:, 72:80]
    s_qf, s_qc, s_sc, s_oh, s_km, s_kc, s_tm, s_tc, s_mv, s_vc = [k.sem(f"{tag}_{n}") for n in
        ("qp", "qp_copied", "scores", "onehot", "kv", "kv_copied", "onehot_T", "onehot_T_copied", "mv", "mv_copied")]
    nq = split.q
    split.late_ring = 2

    def pe_part(pe):
        for c in range(NC_):
            nc.tensor.matmul(k.ps[:, 4 + c, :], k.w["l2x_full"][:, :], k.xnT[:, c * CH:(c + 1) * CH], start=True,
                             stop=True).then_inc(s_qf, 1)
        pe.wait_ge(s_qc, NC_)
        mv_at = lambda b, t: k.ps[:, 2 + b % 2, 8 * t:8 * t + 8]

        def pick(b):
            pe.wait_ge(s_oh, 2 * b + 2)
            if b:
                pe.wait_ge(s_tc, b)
            for m in range(2):
                for t in range(2):
                    mm = nc.tensor.transpose(k.ps[:, 6, m * S + t * P:m * S + (t + 1) * P],
                                             OH[(2 * b + t) % 4][:, m * P:(m + 1) * P], k.ident[:, :])
            mm.then_inc(s_tm, 1)
            pe.wait_ge(s_tc, b + 1)
            pe.wait_ge(s_kc, 2 * b + 2)
            i = nq + b // 2
            if b % 2 == 0:
                split.tensor_ready(pe, i)
            for m in range(2):
                mm = nc.tensor.matmul(split.bank(i)[:, (b % 2) * S:(b % 2 + 1) * S], kv[:, 2 * b + m, 0:P],
                                      OHT[b % 2][:, m, :], start=(m == 0), stop=(m == 1))
            if b % 2:
                mm.then_inc(split.s_mm, 1)
            if b >= 2:
                pe.wait_ge(s_vc, b - 1)
            for t in range(2):
                for m in range(2):
                    mm = nc.tensor.matmul(mv_at(b, t), OHT[b % 2][:, m, t * P:(t + 1) * P], kv[:, 2 * b + m, P:KW],
                                          start=(m == 0), stop=(m == 1))
            mm.then_inc(s_mv, 1)

        for t in range(T):
            if t >= 2:
                pe.wait_ge(s_oh, t - 1)
            b = t // 2
            nc.tensor.matmul(k.ps[:, 4 + t % 2, 0:S], qpT[:, t * P:(t + 1) * P], k.ctxT[:, b * S:(b + 1) * S],
                             start=True, stop=True).then_inc(s_sc, 1)
            if t:
                pe.wait_ge(s_kc, t)
            nc.tensor.matmul(k.ps[:, 7, 0:KW], k.ctxT[:, t * P:(t + 1) * P], k.w["l2x_k"][:, :], start=True,
                             stop=True).then_inc(s_km, 1)
            if t % 2 and t >= 3:
                pick((t - 3) // 2)
        pick(B - 1)

    def act_part(act):
        for c in range(NC_):
            act.wait_ge(s_qf, c + 1)
            nc.scalar.activation(qpT[:, c * CH:(c + 1) * CH], k.ps[:, 4 + c, :], ACT.Copy).then_inc(s_qc, 1)

        def pick(b):
            act.wait_ge(s_tm, b + 1)
            if b >= 2:
                act.wait_ge(s_mv, b - 1)
            nc.scalar.activation(OHT[b % 2].rearrange("p m l -> p (m l)"), k.ps[:, 6, :], ACT.Copy).then_inc(s_tc, 1)
            act.wait_ge(s_mv, b + 1)
            nc.scalar.activation(V[:, 2 * b:2 * b + 2, 0, 0:8], k.ps[:, 2 + b % 2, 0:16].rearrange(
                "p (t e) -> p t e", t=2), ACT.Copy).then_inc(s_vc, 1)
            if b % 2:
                split.scalar(nc, act, nq + b // 2)

        for t in range(T):
            act.wait_ge(s_km, t + 1)
            nc.scalar.activation(kv[:, t, :], k.ps[:, 7, 0:KW], ACT.Copy).then_inc(s_kc, 1)
            if t % 2 and t >= 3:
                pick((t - 3) // 2)
        pick(B - 1)

    def dve_part(dve):
        st = k.dve_steps
        idx_i = k.idx_i[:, 0:8]
        for t in range(T):
            dve.wait_ge(s_sc, t + 1)
            sc = k.ps[:, 4 + t % 2, 0:S]
            st.link(dve, nc.vector.max(top, sc))
            st.link(dve, nc.vector.max_index(idx_i, top, sc))
            st.link(dve, nc.vector.tensor_copy(idx, idx_i))
            if t >= 4:
                dve.wait_ge(s_tm, (t - 4) // 2 + 1)
            nc.vector.tensor_scalar(OH[t % 4], k.iota[:, :], idx[:, 0:1], None, ALU.is_equal).then_inc(s_oh, 1)
            dve.wait_ge(s_oh, t + 1)
            if t % 2 and t >= 5 and ((t - 3) // 2) % 2:
                split.vector(nc, dve, nq + (t - 3) // 4)
        split.vector(nc, dve, nq + (B - 1) // 2)

    return {"pe": pe_part, "act": act_part, "dve": dve_part}


def turn_attn(nc, k, width, dst, s_tp):
    def pe_part(pe):
        for t in range(T):
            nc.tensor.transpose(k.ps[0:width, t // TC, (t % TC) * P:(t % TC + 1) * P], k.attn[:, t, 0:width],
                                k.ident[:, :]).then_inc(s_tp, 1)

    def act_part(act, done):
        for c in range(NC_):
            act.wait_ge(s_tp, TC * (c + 1))
            nc.scalar.activation(dst[:, c * CH:(c + 1) * CH], k.ps[0:width, c, :], ACT.Copy).then_inc(done, 1)
    return pe_part, act_part


def project_out(nc, k, cfg):
    s_tp, s_cp, s_mm = [k.sem(f"{cfg['tag']}_o_{n}") for n in ("tp", "copied", "mm")]
    pe_turn, act_turn = turn_attn(nc, k, P, k.xnT, s_tp)
    with nc.Block() as block:
        @block.tensor
        def _(pe):
            pe_turn(pe)
            for t in range(T):
                if t % TC == 0:
                    pe.wait_ge(s_cp, t // TC + 1)
                nc.tensor.matmul(k.ps[:, 4 + t // TC, (t % TC) * P:(t % TC + 1) * P], k.xnT[:, t * P:(t + 1) * P],
                                 k.w["l2x_c"][:, :], start=True, stop=True).then_inc(s_mm, 1)

        @block.scalar
        def _(act):
            act_turn(act, s_cp)

        @block.vector
        def _(dve):
            for c in range(NC_):
                dve.wait_ge(s_mm, TC * (c + 1))
                xs = k.x[:, TC * c:TC * (c + 1), :]
                nc.vector.scalar_tensor_tensor(xs, k.ps[:, 4 + c, :].rearrange("p (t d) -> p t d", d=D),
                                               k.tanh_g[:, 4:5], xs, ALU.mult, ALU.add)


def project_latent(nc, k, cfg):
    s_tp, s_cp, s_mm = [k.sem(f"{cfg['tag']}_o_{n}") for n in ("tp", "copied", "mm")]
    LAT = NHEAD * cfg["dv"]
    aoT = k.V[0:LAT, 0:N]
    pe_turn, act_turn = turn_attn(nc, k, LAT, aoT, s_tp)
    with nc.Block() as block:
        @block.tensor
        def _(pe):
            pe_turn(pe)
            for c in range(NC_):
                pe.wait_ge(s_cp, c + 1)
                nc.tensor.matmul(k.ps[:, 4 + c, :], k.w["l2m_o"][0:LAT, :], aoT[:, c * CH:(c + 1) * CH], start=True,
                                 stop=True).then_inc(s_mm, 1)

        @block.scalar
        def _(act):
            act_turn(act, s_cp)
            for c in range(NC_):
                act.wait_ge(s_mm, c + 1)
                nc.scalar.activation(k.xnT[:, c * CH:(c + 1) * CH], k.ps[:, 4 + c, :], ACT.Identity,
                                     bias=k.w["l2m_ob"][:, 0:1])


A2 = dict(tag="l2x", kd=8, dv=8, scale=float(1 / np.sqrt(8.0)), mqa=True, self=False, select=select_kv, finish=project_out)
A2M = dict(tag="l2m", kd=4, dv=4, scale=0.5, mqa=False, self=True, finish=project_latent)
A1 = dict(tag="l1x", kd=8, dv=8, scale=float(1 / np.sqrt(8.0)), mqa=False, self=False, add=2)
A3 = dict(tag="l3x", kd=8, dv=8, scale=float(1 / np.sqrt(128.0)), mqa=False, self=False, add=6)


def attend(cfg):
    return lambda nc, k: attention(nc, k, cfg)



def program(nc, d, out, stages=99):
    with ExitStack() as ctx:
        k = Ctx()
        k.d = d
        k.ln_calls = 0

        def sb(name, shape, dt=F32):
            return ctx.enter_context(nc.sbuf_tensor(name, shape, dt))

        def sem(name):
            return ctx.enter_context(nc.semaphore(name))

        stage_sems = []

        def stage_sem(name):
            handle = nc.alloc_semaphore(name=name)
            stage_sems.append(handle)
            return handle

        def retire_stage_sems():
            with nc.Block() as block:
                @block.gpsimd
                def _(pool):
                    for handle in stage_sems:
                        nc.gpsimd.sem_clear(handle)
            for handle in stage_sems:
                nc.release_semaphore(handle)
            stage_sems.clear()

        k.sem = stage_sem
        k.x, k.xn = sb("x", [P, T, D]), sb("xn", [P, T, D])
        k.xnT, k.ctxT = sb("xnT", [P, N]), sb("ctxT", [P, N])
        k.attn = sb("attn", [P, T, D])
        k.V = sb("V", [P, T * 16 * 9])
        k.Qs = sb("Qs", [P, 4, N], F16)
        k.Kst = sb("Kst", [P, 2, N], F16)
        k.big = sb("big", [P, 16 * N // 2])
        k.P4 = sb("P4", [P, 4 * 1024])
        k.misc = sb("misc", [P, 2048])
        k.small = sb("small", [P, 512])
        k.zeros = sb("zeros", [P, S])
        k.Qaug = sb("Qaug", [P, 2, S], F16)
        k.OT = sb("OT", [P, 2, S])
        k.NM = sb("NM", [P, 2, 2, P], F16)
        k.stats, k.mv = sb("stats", [P, T, 6]), sb("mv", [P, T, 2])
        k.std, k.rstd = sb("std", [P, T]), sb("rstd", [P, T])
        k.ident, k.identh, k.identb = sb("ident", [P, P]), sb("identh", [P, P], F16), sb("identb", [P, P], BF16)
        k.cmask = sb("cmask", [P, S + P], BF16)
        k.sel32 = k.big[0:32, 0:32 * P]
        k.G = sb("G", [P, T, 36])
        k.idx_i = sb("idx_i", [P, 8 * T], U32)
        k.acc = sb("acc", [P, CH])
        k.aux = k.Qs[:, :, :].rearrange("p g n -> p (g n)").bitcast(F32)
        k.hi = sb("hi", [P, 2, CH], F16)
        k.junk, k.pjunk = sb("junk", [P, 8]), sb("pjunk", [P, 8])
        k.iota = sb("iota", [P, S])
        k.consts = sb("consts", [P, 8])
        k.gates_raw, k.tanh_g = sb("gates_raw", [P, 8]), sb("tanh_g", [P, 8])
        k.ps = ctx.enter_context(nc.psum_tensor("ps", [P, 8, CH], F32))
        k.w = {n: sb("w_" + n, list(d[n].shape)) for n in SMALL_WEIGHTS}
        k.ln_var, k.ln_std, k.ln_xn, k.ln_tp = sem("ln_var"), sem("ln_std"), sem("ln_xn"), sem("ln_tp")
        k.setup_in, k.ctx_tp, k.out_done = sem("setup_in"), sem("ctx_tp"), sem("out_done")
        k.aux_in, k.w_in = sem("aux_in"), [sem(f"w_in{q}") for q in range(4)]
        k.aux_n = k.w_n = 0
        k.dve_steps, k.act_steps = Steps(sem("dve_steps")), Steps(sem("act_steps"))

        setup(nc, k)
        plan = STAGES[:stages]
        for n, stage in enumerate(plan):
            if n and n % 4 == 0:
                retire_stage_sems()
            layer_norm(nc, k)
            stage(nc, k)
        with nc.Block() as block:
            @block.sync
            def _(sp):
                sp.dma_start(out.rearrange("(t p) d -> p t d", p=P), k.x[:, :, :]).then_inc(k.out_done, 16)
                sp.wait_ge(k.out_done, 16)


SMALL_WEIGHTS = ["l0_gate", "l0_gbias", "l0_rms", "ones", "l1x_q", "l1x_k", "l1x_v", "l3x_q", "l3x_k", "l3x_v", "l3x_b", "l3x_bv",
                 "l2m_q", "l2m_k", "l2m_v", "l2m_b", "l2m_bv", "l2m_o", "l2m_ob", "l2x_q", "l2x_k", "l2x_full", "l2x_c"]
def latent_ffn(nc, k):
    attention(nc, k, A2M)
    ffn(CFG2)(nc, k)


STAGES = [mlstm, ffn(CFG0), attend(A1), ffn(CFG1), attend(A2), latent_ffn, attend(A3), ffn(CFG3)]



def constants():
    c = {}
    c["ident"] = np.eye(P, dtype=np.float32)
    c["identh"] = np.eye(P, dtype=np.float16)
    key, qry = np.arange(P)[:, None], np.arange(P)[None, :]
    tri = np.where(qry < key, NEG, 0.0)
    c["cmask"] = np.concatenate([tri, np.zeros((P, P)), tri], 1).astype(np.float32)
    c["iota"] = np.broadcast_to(np.arange(S, dtype=np.float32), (P, S)).copy()
    sel = np.zeros((32, 32, P), np.float32)
    sel[np.arange(32), np.arange(32)] = 1.0
    c["sel32"] = sel.reshape(32, 32 * P)
    cons = np.zeros((P, 8), np.float32)
    row = np.arange(P) % BLK - 2
    for i, (kd, lo) in enumerate(((8, 2), (8, 1), (4, 2), (4, 1))):
        cons[:, i] = np.where((row >= lo * kd) & (row < (lo + 1) * kd), -1.0, 0.0)
    c["consts"] = cons
    return c


def layouts(i):
    o = {}
    f = lambda a: np.ascontiguousarray(a, dtype=np.float32)
    o["x"], o["ctx"] = f(i["x"]).reshape(N, D), f(i["ctx_1024"]).reshape(N, D)
    g = np.stack([f(i["g_xattn"]), f(i["g_ffn"])], 1).reshape(1, 8)
    o["g_all"] = np.repeat(g, P, 0)
    w = np.zeros((P, 3, 92), np.float32)
    for n, name in enumerate(("igate", "fgate")):
        w[:, :, 28 + 32 * n:32 + 32 * n] = f(i[f"L0_xattn_{name}_kernel"]).reshape(3, D, 4).transpose(1, 0, 2)
    o["l0_gate"] = w.reshape(P, 3 * 92)
    b = np.zeros((P, 2), np.float32)
    for n, name in enumerate(("igate", "fgate")):
        b[0:32, n] = np.tile(f(i[f"L0_xattn_{name}_bias"]), 8)
    o["l0_gbias"] = b
    o["l0_rms"] = np.broadcast_to(np.tile(f(i["L0_xattn_rms_scale"]), 4), (P, D)).copy()
    def rows(a):
        return np.concatenate([f(a), np.zeros((P - a.shape[0], a.shape[1]), np.float32)], 0)

    def spread(a):
        return np.repeat(f(a).reshape(1, -1), P, 0)

    def hidden_cols(a):
        return f(a).reshape(-1, P).T

    def tile_rows(a):
        e, ff, dd = a.shape
        return f(a).reshape(e, ff // P, P, dd).transpose(2, 0, 1, 3).reshape(P, e, -1)

    def cat(*parts):
        return np.concatenate(parts, 2).reshape(P, -1)

    tr = lambda a: f(a).transpose(2, 0, 1)
    o["l0f_aux"] = np.concatenate([f(i["L0_ffn_router_w"]), hidden_cols(i["L0_ffn_b1"]), spread(i["L0_ffn_gamma"]),
                                   spread(i["L0_ffn_b2"]), rows(i["L0_ffn_beta"])], 1)
    o["l0f_w"] = cat(f(i["L0_ffn_w1"]).transpose(1, 0, 2), tile_rows(i["L0_ffn_w2"]))
    o["l1f_aux"] = np.concatenate([f(i["L1_ffn_router_w"]).T, spread(i["L1_ffn_router_bias"])], 1)
    four = lambda a: f(a).reshape(4, P, D)
    o["l1f_w"] = cat(*(np.concatenate([x, y], 1) for x, y in (
        (tr(i["L1_ffn_gate_w"]), tr(four(i["L1_ffn_sgate_w"]))), (tr(i["L1_ffn_up_w"]), tr(four(i["L1_ffn_sup_w"]))),
        (tr(i["L1_ffn_down_w"]), f(i["L1_ffn_sdown_w"]).T.reshape(4, P, D).transpose(1, 0, 2)))))
    o["l2f_aux"] = np.concatenate([f(i["L2_ffn_router_w"]), spread(i["L2_ffn_router_b"]), hidden_cols(i["L2_ffn_b1"]),
                                   rows(i["L2_ffn_b2"])], 1)
    o["l2f_w"] = cat(f(i["L2_ffn_w1"]).transpose(1, 0, 2), tile_rows(i["L2_ffn_w2"]))
    o["l3f_aux"] = np.concatenate([f(i["L3_ffn_gate_w"]).T, spread(i["L3_ffn_lb_bias"])], 1)
    o["l3f_w"] = cat(*(np.concatenate([tr(x), f(y).T[:, None, :]], 1) for x, y in (
        (i["L3_ffn_w1"], i["L3_ffn_cfc"]), (i["L3_ffn_w2"], i["L3_ffn_cproj"]))))

    def blocks(a, kd):
        a = f(a).reshape(a.shape[0], -1, kd)
        z = np.zeros(a.shape[:2] + (BLK,), np.float32)
        for r in range(3):
            z[:, :, 2 + r * kd:2 + (r + 1) * kd] = a
        return z.reshape(a.shape[0], -1)

    def bias_cols(q, kk, kd):
        return np.concatenate([blocks(np.asarray(v).reshape(1, -1), kd).reshape(-1, P).T for v in (q, kk)], 1)

    o["ones"] = np.ones((P, P), np.float32)
    o["l1x_q"], o["l1x_k"] = blocks(f(i["L1_xattn_Wq"]).T, 8), blocks(f(i["L1_xattn_Wk"]).T, 8)
    o["l1x_v"] = f(i["L1_xattn_Wv"]).T
    o["l3x_q"], o["l3x_k"], o["l3x_v"] = blocks(i["L3_xattn_Wq"], 8), blocks(i["L3_xattn_Wk"], 8), f(i["L3_xattn_Wv"])
    o["l3x_b"], o["l3x_bv"] = bias_cols(i["L3_xattn_bq"], i["L3_xattn_bk"], 8), spread(i["L3_xattn_bv"])
    four_of_8 = lambda a: f(a).reshape(-1, 16, 8)[:, :, 0:4].reshape(-1, 64)
    o["l2m_q"], o["l2m_k"], o["l2m_v"] = blocks(four_of_8(i["L2_ffn_q_w"]), 4), blocks(i["L2_ffn_k_w"], 4), f(i["L2_ffn_v_w"])
    o["l2m_b"], o["l2m_bv"] = bias_cols(four_of_8(i["L2_ffn_q_b"]), i["L2_ffn_k_b"], 4), spread(i["L2_ffn_v_b"])
    o["l2m_o"], o["l2m_ob"] = f(i["L2_ffn_o_w"]), f(i["L2_ffn_o_b"]).reshape(P, 1)
    wkv = f(i["L2_xattn_Wkv"]).T
    o["l2x_q"] = blocks(f(i["L2_xattn_Wq"]).T, 8)
    o["l2x_k"] = np.concatenate([blocks(np.tile(wkv[:, 0:8], (1, HG)), 8), wkv[:, 8:16]], 1)
    o["l2x_full"], o["l2x_c"] = f(i["L2_xattn_Wq"]).T, f(i["L2_xattn_Wc"]).T
    return o


def kernel(**inputs):
    import concourse.bacc as _bacc
    from concourse.bass_utils import run_bass_kernel_spmd as _run

    nc = _bacc.Bacc("TRN2", target_bir_lowering=False, num_devices=1)
    arrays, d = {}, {}
    for name, a in {**constants(), **layouts(inputs)}.items():
        a = np.ascontiguousarray(a)
        arrays[f"in_{name}"] = a
        d[name] = nc.dram_tensor(f"in_{name}", a.shape, mybir.dt.from_np(a.dtype), kind="ExternalInput").ap()
    out = nc.dram_tensor("out_x", (N, D), F32, kind="ExternalOutput").ap()
    program(nc, d, out)
    r = _run(nc, [arrays], core_ids=[0])
    return r.results[0]["out_x"].reshape(B, S, D)
```

```python
from contextlib import ExitStack

import numpy as np

import concourse.bass as bass
from concourse import mybir

F32 = mybir.dt.float32
F16 = mybir.dt.float16
BF16 = mybir.dt.bfloat16
U32 = mybir.dt.uint32
ALU = mybir.AluOpType
ACT = mybir.ActivationFunctionType
X_AXIS = mybir.AxisListType.X

P = 128
B, S, D = 8, 256, 128
N = B * S
T = N // P
CH = 512
NC_ = N // CH
TC = CH // P
BLK = 32
HG = P // BLK
SHIFT = 1024.0
SHIFT_PAIR = float(np.full(2, SHIFT, np.float16).view(np.float32)[0])
NEG = -1e30
LN_EPS = 1e-5


class Steps:

    def __init__(self, sem):
        self.sem, self.n = sem, 0

    def inc(self, ins):
        ins.then_inc(self.sem, 1)
        self.n = self.n + 1

    def link(self, eng, ins):
        self.inc(ins)
        eng.wait_ge(self.sem, self.n)


class Ctx:
    pass



def layer_norm(nc, k, loads=None, zeroed=0, weights=None):
    k.ln_calls += 1
    c0 = k.ln_calls - 1
    with nc.Block() as block:
        if loads is not None:
            @block.sync
            def _(sp):
                loads(sp)

        @block.gpsimd
        def _(pool):
            if zeroed:
                nc.gpsimd.memset(k.big[:, 0:zeroed], 0.0)
            if weights is not None:
                weights.first_hi(nc, pool)

        @block.vector
        def _(dve):
            st = k.dve_steps
            for t in range(T):
                st.inc(nc.vector.bn_stats(k.stats[:, t, :], k.x[:, t, :]))
            dve.wait_ge(st.sem, st.n)
            for t in range(T):
                st.inc(nc.vector.bn_aggr(k.mv[:, t, :], k.stats[:, t, :]))
            dve.wait_ge(st.sem, st.n)
            nc.vector.tensor_scalar(k.std[:, :], k.mv[:, :, 1], LN_EPS, None, ALU.add).then_inc(k.ln_var, 1)
            dve.wait_ge(k.ln_std, c0 + 1)
            st.link(dve, nc.vector.reciprocal(k.rstd[:, :], k.std[:, :]))
            for t in range(T):
                nc.vector.tensor_scalar(k.xn[:, t, :], k.x[:, t, :], k.mv[:, t, 0:1], k.rstd[:, t:t + 1],
                                        ALU.subtract, ALU.mult).then_inc(k.ln_xn, 1)

        @block.tensor
        def _(pe):
            for t in range(T):
                pe.wait_ge(k.ln_xn, c0 * T + t + 1)
                nc.tensor.transpose(k.ps[:, t // TC, (t % TC) * P:(t % TC + 1) * P], k.xn[:, t, :],
                                    k.ident[:, :]).then_inc(k.ln_tp, 1)

        @block.scalar
        def _(act):
            act.wait_ge(k.ln_var, c0 + 1)
            nc.scalar.activation(k.std[:, :], k.std[:, :], ACT.Sqrt).then_inc(k.ln_std, 1)
            for c in range(NC_):
                act.wait_ge(k.ln_tp, c0 * T + TC * (c + 1))
                nc.scalar.activation(k.xnT[:, c * CH:(c + 1) * CH], k.ps[:, c, :], ACT.Copy)



def setup(nc, k):
    loads = [(k.attn[:, :, :], k.d["ctx"].rearrange("(t p) d -> p t d", p=P)),
             (k.ident[:, :], k.d["ident"]), (k.gates_raw[:, :], k.d["g_all"]),
             (k.misc[:, 0:S + P], k.d["cmask"]),
             (k.x[:, :, :], k.d["x"].rearrange("(t p) d -> p t d", p=P))]
    with nc.Block() as block:
        @block.sync
        def _(sp):
            for dst, src in loads:
                sp.dma_start(dst, src).then_inc(k.setup_in, 16)

        @block.tensor
        def _(pe):
            pe.wait_ge(k.setup_in, 16 * len(loads))
            for t in range(T):
                nc.tensor.transpose(k.ps[:, t // TC, (t % TC) * P:(t % TC + 1) * P], k.attn[:, t, :],
                                    k.ident[:, :]).then_inc(k.ctx_tp, 1)

        @block.scalar
        def _(act):
            act.wait_ge(k.setup_in, 16 * len(loads))
            nc.scalar.activation(k.tanh_g[:, :], k.gates_raw[:, :], ACT.Tanh)
            for c in range(NC_):
                act.wait_ge(k.ctx_tp, TC * (c + 1))
                nc.scalar.activation(k.ctxT[:, c * CH:(c + 1) * CH], k.ps[:, c, :], ACT.Copy)

        @block.gpsimd
        def _(pool):
            nc.gpsimd.memset(k.sel[:, :], 0.0).then_inc(k.sel_zero, 1)
            nc.gpsimd.memset(k.NM[:, :, :, :], 0.0)
            nc.gpsimd.memset(k.keys[:, :], 0.0)
            nc.gpsimd.memset(k.misc[:, 6 * S:7 * S], 0.0)

        @block.vector
        def _(dve):
            dve.wait_ge(k.setup_in, 16 * len(loads))
            nc.vector.tensor_copy(k.cmask[:, :], k.misc[:, 0:S + P])
            nc.vector.tensor_copy(k.identb[:, :], k.ident[:, :])


def load_first(k, sp):
    loads = [(k.w[n][:], k.d[n]) for n in k.w if n.startswith("l0")] + [(k.identh[:, :], k.d["identh"])]
    k.first_n = 16 * (len(loads) + 1)
    for dst, src in loads:
        sp.dma_start(dst, src).then_inc(k.first_in, 16)
    sp.wait_ge(k.sel_zero, 1)
    sp.dma_start(k.sel32[:, :], k.d["sel32"]).then_inc(k.first_in, 16)


def load_rest(k, sp):
    loads = [(k.consts[:, :], k.d["consts"]), (k.iota[:, :], k.d["iota"])]
    loads += [(k.w[n][:], k.d[n]) for n in k.w if not n.startswith("l0")]
    k.rest_n = 16 * len(loads)
    for dst, src in loads:
        sp.dma_start(dst, src).then_inc(k.rest_in, 16)


def await_loads(nc, loaded, count):
    with nc.Block() as block:
        @block.tensor
        def _(pe):
            pe.wait_ge(loaded, count)

        @block.scalar
        def _(act):
            act.wait_ge(loaded, count)

        @block.gpsimd
        def _(pool):
            pool.wait_ge(loaded, count)

        @block.vector
        def _(dve):
            dve.wait_ge(loaded, count)



def mlstm(nc, k):
    NH, HD = 4, 32
    R = B * NH
    W3 = S + P
    SC = float(1.0 / np.sqrt(HD))
    wide = k.P4
    g_ = [k.misc[0:R, i * S:(i + 1) * S] for i in range(8)]
    f_, nf, ex, cs, a_, M_, nM, em = g_
    aT, emT = k.small[:, 0:2 * R].rearrange("p (t r) -> p t r", t=2), k.small[:, 64:64 + 2 * R].rearrange("p (t r) -> p t r", t=2)
    ss = k.small[:, 128:128 + T * NH]
    Vm = k.V[:, 0:T * NH * (HD + 1)].rearrange("p (t h e) -> p t h e", t=T, h=NH)
    wg = k.w["l0_gate"][:, :].rearrange("p (c n) -> p c n", c=3)
    gb = k.w["l0_gbias"]
    dT = [wide[:, i * W3:(i + 1) * W3] for i in range(2)]
    cT = [wide[:, (2 + i) * W3:(3 + i) * W3] for i in range(2)]
    nrm = wide[:, 4 * W3:4 * W3 + 64]
    rms = wide[:, 4 * W3 + 64:4 * W3 + 192]
    sq = wide[:, 4 * W3 + 192:4 * W3 + 448]
    s_w, s_g, s_ps, s_f, s_tp, s_st, s_L, s_d, s_c, s_o, s_nrm, s_v, s_var, s_std = [
        k.sem("l0_" + n) for n in ("gate_w", "gate_mm", "gate_act", "gate_dve", "gate_tp", "scores", "logdecay",
                                   "decay", "weighted", "out", "normed", "values", "var", "std")]
    s_tt, s_keys = k.sem("l0_gate_cols"), k.sem("l0_keys")
    nM_rows = k.misc[:, 6 * S:7 * S]
    keys = k.keys.rearrange("p (h n) -> p h n", h=NH)

    def copy_keys(h, copy):
        hs = slice(HD * h, HD * h + HD)
        copy(keys[hs, h, :], k.ctxT[hs, :]).then_inc(s_keys, 1)

    def normalise(dve, st, b):
        o = k.ps[:, 4 + b % 2, 0:2 * NH * (HD + 1)].rearrange("p (t h e) -> p t h e", t=2, h=NH)
        n = nrm[:, 0:2 * NH].rearrange("p (t h) -> p t h", t=2)
        dve.wait_ge(s_o, NH * (b + 1))
        st.link(dve, nc.vector.tensor_tensor(n, o[:, :, :, HD], emT[:, :, NH * b:NH * b + NH], ALU.max))
        st.link(dve, nc.vector.tensor_scalar(n, n, 1e-6, None, ALU.add))
        st.link(dve, nc.vector.reciprocal(n, n))
        at = k.attn[:, 2 * b:2 * b + 2, :].rearrange("p t (h e) -> p t h e", h=NH)
        ins = nc.vector.tensor_tensor(at, o[:, :, :, 0:HD], n.unsqueeze(3).to_broadcast([P, 2, NH, HD]), ALU.mult)
        ins.then_inc(s_nrm, 1)
        dve.wait_ge(s_nrm, b + 1)
        st.link(dve, nc.vector.tensor_tensor(sq.rearrange("p (t e) -> p t e", t=2), k.attn[:, 2 * b:2 * b + 2, :],
                                             k.attn[:, 2 * b:2 * b + 2, :], ALU.mult))
        st.link(dve, nc.vector.tensor_reduce(ss[:, 2 * NH * b:2 * NH * (b + 1)],
                                             sq.rearrange("p (g e) -> p g e", e=HD), X_AXIS, ALU.add))

    with nc.Block() as block:
        @block.sync
        def _(sp):
            for t in range(T):
                sp.dma_start(Vm[:, t, :, 0:HD], k.d["ctx"][t * P:(t + 1) * P, :].rearrange("p (h e) -> p h e", h=NH)
                             ).then_inc(s_v, 16)
            load_rest(k, sp)

        @block.gpsimd
        def _(pool):
            nc.gpsimd.memset(Vm[:, :, :, HD:HD + 1], 1.0).then_inc(s_v, 1)

        @block.tensor
        def _(pe):
            pe.wait_ge(s_w, 1)
            out = k.ps[0:2 * R, 6, 0:S]
            for b in range(B):
                w0 = NH * (B - 1 - b)
                for c, src in ((0, k.xnT), (1, k.ctxT)):
                    mm = nc.tensor.matmul(out, wg[:, c, w0:w0 + 2 * R], src[:, b * S:(b + 1) * S],
                                          start=(b == 0 and c == 0), stop=(b == B - 1 and c == 1))
            mm.then_inc(s_g, 1)
            pe.wait_ge(s_f, 2)
            for i, src in enumerate((a_, em)):
                for t in range(2):
                    mm = nc.tensor.transpose(k.ps[:, 7, 64 * i + 32 * t:64 * i + 32 * t + 32],
                                             src[:, t * P:(t + 1) * P], k.ident[0:R, 0:R])
            mm.then_inc(s_tp, 1)

            def scores(r):
                b, h = divmod(r, NH)
                if r >= 2:
                    pe.wait_ge(s_c, r - 1)
                st, lg = k.ps[:, r % 2, :], k.ps[:, 2 + r % 2, :]
                nc.tensor.matmul(st[:, 0:S], keys[:, h, b * S:b * S + P], k.xnT[:, b * S:(b + 1) * S], start=True, stop=True)
                nc.tensor.matmul(st[:, S:W3], keys[:, h, b * S + P:(b + 1) * S], k.xnT[:, b * S + P:(b + 1) * S],
                                 start=True, stop=True).then_inc(s_st, 1)
                if r >= 2:
                    pe.wait_ge(s_d, r - 1)
                nc.tensor.matmul(lg[:, 0:W3], k.identb[:, :], k.cmask[:, :], start=True, stop=False, skip_group_check=True)
                sel = k.sel[:, r * P:(r + 1) * P]
                nc.tensor.matmul(lg[:, 0:S], sel, nM_rows[:, :], start=False, stop=False, skip_group_check=True)
                nc.tensor.matmul(lg[:, S:W3], sel, nM_rows[:, P:S], start=False, stop=True,
                                 skip_group_check=True).then_inc(s_L, 1)

            def weigh(r):
                b, h = divmod(r, NH)
                pe.wait_ge(s_c, r + 1)
                if h == 0 and b >= 2:
                    pe.wait_ge(s_nrm, b - 1)
                o = k.ps[:, 4 + b % 2, 0:2 * NH * (HD + 1)].rearrange("p (t h e) -> p t h e", t=2, h=NH)
                c = cT[r % 2]
                nc.tensor.matmul(o[:, 0, h, :], c[:, 0:P], Vm[:, 2 * b, h, :], start=True, stop=True)
                nc.tensor.matmul(o[:, 1, h, :], c[:, P:S], Vm[:, 2 * b, h, :], start=True, stop=False)
                nc.tensor.matmul(o[:, 1, h, :], c[:, S:W3], Vm[:, 2 * b + 1, h, :], start=False, stop=True).then_inc(s_o, 1)

            pe.wait_ge(s_f, 3)
            pe.wait_ge(s_keys, NH)
            pe.wait_ge(s_v, 16 * T + 1)
            for r in range(R + 1):
                if r < R:
                    scores(r)
                if r:
                    weigh(r - 1)

        @block.scalar
        def _(act):
            st = k.act_steps
            for h in (0, 1):
                copy_keys(h, lambda dst, src: nc.scalar.activation(dst, src, ACT.Copy))
            act.wait_ge(s_g, 1)
            st.link(act, nc.scalar.activation(f_[:, :], k.ps[R:2 * R, 6, 0:S], ACT.Identity, bias=gb[0:R, 1:2]))
            nc.scalar.activation(nf[:, :], f_[:, :], ACT.Abs).then_inc(s_ps, 1)
            act.wait_ge(s_ps, 1)
            st.link(act, nc.scalar.activation(ex[:, :], nf[:, :], ACT.Exp, scale=-1.0))
            nc.scalar.activation(cs[:, :], ex[:, :], ACT.Ln, bias=1.0).then_inc(s_ps, 1)
            act.wait_ge(s_f, 1)
            nc.scalar.activation(em[:, :], M_[:, :], ACT.Exp, scale=-1.0).then_inc(s_f, 1)
            act.wait_ge(s_tt, 1)
            for r in range(R):
                act.wait_ge(s_L, r + 1)
                if r >= 2:
                    act.wait_ge(s_c, r - 1)
                lg = k.ps[:, 2 + r % 2, :]
                nc.scalar.activation(dT[r % 2][:, 0:S], lg[:, 0:S], ACT.Exp, bias=aT[:, 0, r:r + 1])
                nc.scalar.activation(dT[r % 2][:, S:W3], lg[:, S:W3], ACT.Exp, bias=aT[:, 1, r:r + 1]).then_inc(s_d, 1)
            act.wait_ge(s_var, 1)
            nc.scalar.activation(ss, ss, ACT.Sqrt).then_inc(s_std, 1)

        @block.vector
        def _(dve):
            st = k.dve_steps
            nc.vector.tensor_tensor(wg[:, 1], wg[:, 1], wg[:, 2], ALU.add).then_inc(s_w, 1)
            for h in (2, 3):
                copy_keys(h, nc.vector.tensor_copy)
            st.link(dve, nc.vector.memset(k.zeros[0:R, 0:S], 0.0))
            dve.wait_ge(s_ps, 2)
            st.link(dve, nc.vector.scalar_tensor_tensor(ex[:, :], f_[:, :], 0.0, cs[:, :], ALU.min, ALU.subtract))
            st.link(dve, nc.vector.tensor_tensor_scan(cs[:, :], ex[:, :], k.zeros[0:R, 0:S], 0.0, ALU.add, ALU.add))
            st.link(dve, nc.vector.scalar_tensor_tensor(a_[:, :], k.ps[0:R, 6, 0:S], gb[0:R, 0:1], cs[:, :], ALU.add, ALU.subtract))
            st.link(dve, nc.vector.tensor_tensor_scan(nf[:, :], a_[:, :], a_[:, :], -3e38, ALU.max, ALU.max))
            nc.vector.tensor_tensor(M_[:, :], cs[:, :], nf[:, :], ALU.add).then_inc(s_f, 1)
            dve.wait_ge(s_f, 2)
            nc.vector.tensor_scalar(nM[:, :], nf[:, :], -1.0, None, ALU.mult).then_inc(s_f, 1)
            dve.wait_ge(s_tp, 1)
            nc.vector.tensor_copy(k.small[:, 0:128], k.ps[:, 7, 0:128]).then_inc(s_tt, 1)
            for r in range(R):
                b, h = divmod(r, NH)
                dve.wait_ge(s_st, r + 1)
                dve.wait_ge(s_d, r + 1)
                if r >= 2:
                    dve.wait_ge(s_o, r - 1)
                nc.vector.scalar_tensor_tensor(cT[r % 2][:, :], k.ps[:, r % 2, 0:W3], SC, dT[r % 2][:, :],
                                               ALU.mult, ALU.mult).then_inc(s_c, 1)
                if h == 0 and b:
                    normalise(dve, st, b - 1)
            normalise(dve, st, B - 1)
            st.link(dve, nc.vector.tensor_scalar(ss, ss, 1.0 / HD, 1e-6, ALU.mult, ALU.add))
            nc.vector.tensor_scalar(rms, k.w["l0_rms"][:, :], 1.0, None, ALU.add).then_inc(s_var, 1)
            dve.wait_ge(s_std, 1)
            st.link(dve, nc.vector.reciprocal(ss, ss))
            at = k.attn[:, :, :].rearrange("p t (h e) -> p t h e", h=NH)
            st.link(dve, nc.vector.tensor_tensor(at, at, ss.rearrange("p (t h) -> p t h", h=NH).unsqueeze(3).to_broadcast([P, T, NH, HD]), ALU.mult))
            st.link(dve, nc.vector.tensor_tensor(k.attn[:, :, :], k.attn[:, :, :], rms.unsqueeze(1).to_broadcast([P, T, D]), ALU.mult))
            st.link(dve, nc.vector.scalar_tensor_tensor(k.x[:, :, :], k.attn[:, :, :], k.tanh_g[:, 0:1], k.x[:, :, :], ALU.mult, ALU.add))



def aux_views(k, spec):
    out, at = {}, 0
    for name, width in spec:
        out[name] = k.aux[:, at:at + width]
        at += width
    return out


class Weights:

    LIFT = 2048.0
    STAGE = 1024

    def __init__(self, k, cfg):
        self.k, self.cfg = k, cfg
        E, self.nub, nf = cfg["E"], cfg["nub"], cfg["nf"]
        self.dn = E * nf * P
        self.up = E * self.nub * P
        half = k.big[:, self.dn:self.dn + self.up].bitcast(F16)
        self.hi, self.lo = half[:, 0:self.up], half[:, self.up:2 * self.up]
        self.experts = cfg["piece"]
        self.cols = self.experts * self.nub * P
        self.pieces = E // self.experts
        end = 16 * N // 2
        self.ring = [k.big[:, end - (i + 1) * self.STAGE:end - (i + 1) * self.STAGE + self.cols] for i in range(2)]
        assert self.pieces * self.experts == E and self.cols <= self.STAGE and self.dn + self.up <= end - 2 * self.STAGE
        self.s_in = [k.sem(f"{cfg['tag']}_piece_in{i}") for i in range(2)]
        self.s_hi, self.s_rest, self.s_done = [k.sem(f"{cfg['tag']}_piece_{n}") for n in ("hi", "rest", "split")]

    def load(self, sp, p):
        if p >= 2:
            sp.wait_ge(self.s_done, p - 1)
        sp.dma_start(self.ring[p % 2], self.k.d[self.cfg["tag"] + "_up"][:, p * self.cols:(p + 1) * self.cols]
                     ).then_inc(self.s_in[p % 2], 16)

    def make_hi(self, nc, act, p):
        act.wait_ge(self.s_in[p], 16)
        nc.scalar.activation(self.hi[:, p * self.cols:(p + 1) * self.cols], self.ring[p], ACT.Copy).then_inc(self.s_hi, 1)

    def first_hi(self, nc, pool):
        pool.wait_ge(self.s_in[0], 16)
        nc.gpsimd.tensor_copy(self.hi[:, 0:self.cols], self.ring[0]).then_inc(self.s_hi, 1)

    def split(self, nc, pool, p):
        cols, w = slice(p * self.cols, (p + 1) * self.cols), self.ring[p % 2]
        if p >= 2:
            pool.wait_ge(self.s_in[p % 2], 16 * (p // 2 + 1))
            nc.gpsimd.tensor_copy(self.hi[:, cols], w).then_inc(self.s_hi, 1)
        pool.wait_ge(self.s_hi, p + 1)
        nc.gpsimd.tensor_tensor(w, w, self.hi[:, cols], ALU.subtract).then_inc(self.s_rest, 1)
        pool.wait_ge(self.s_rest, p + 1)
        nc.gpsimd.tensor_scalar(self.lo[:, cols], w, self.LIFT, None, ALU.mult).then_inc(self.s_done, 1)

    def down(self, e, f):
        at = (e * self.cfg["nf"] + f) * P
        return self.k.big[:, at:at + P]

    def up_cols(self, e, f):
        at = (e * self.nub + f) * P
        return slice(at, at + P)


def load_layer(nc, k, cfg, sp):
    tag, E, per = cfg["tag"], cfg["E"], cfg["nf"] * P
    width = k.d[tag + "_aux"].shape[1]
    sp.dma_start(k.aux[:, 0:width], k.d[tag + "_aux"]).then_inc(k.aux_in, 16)
    k.aux_n += 1
    k.w_n += 1
    for p in range(2):
        cfg["weights"].load(sp, p)
    for q in range(4):
        a, b = E * q // 4 * per, E * (q + 1) // 4 * per
        sp.dma_start(k.big[:, a:b], k.d[tag + "_dn"][:, a:b]).then_inc(k.w_in[q], 16)


def route(nc, k, cfg, loaded):
    tag, E, K = cfg["tag"], cfg["route_E"], cfg["K"]
    kind = cfg["route"]
    src = cfg["src"](k)
    a = aux_views(k, cfg["aux"])
    L = k.misc[:, 0:T * E].rearrange("p (t e) -> p t e", e=E)
    Lb = k.misc[:, 512:512 + T * E].rearrange("p (t e) -> p t e", e=E)
    eq = k.misc[:, 1024:1024 + T * E].rearrange("p (t e) -> p t e", e=E)
    tmp = k.misc[:, 1536:1536 + T * E].rearrange("p (t e) -> p t e", e=E)
    top = k.small[:, 0:8 * T].rearrange("p (t j) -> p t j", j=8)
    idx = k.small[:, 8 * T:16 * T].rearrange("p (t j) -> p t j", j=8)
    w = k.small[:, 16 * T:(16 + K) * T].rearrange("p (t j) -> p t j", j=K)
    one = k.small[:, 24 * T:25 * T]
    idx_i = k.idx_i[:, :].rearrange("p (t j) -> p t j", j=8)
    G = k.G[:, :, 0:E]
    s_mm, s_arg, s_exp = [k.sem(f"{tag}_r_{n}") for n in ("logits", "exp_arg", "exp")]
    weights = cfg["weights"]
    s_xh = k.sem(f"{tag}_x_hi")
    with nc.Block() as block:
        @block.gpsimd
        def _(pool):
            weights.split(nc, pool, 0)
            weights.split(nc, pool, 1)

        if not loaded:
            @block.sync
            def _(sp):
                load_layer(nc, k, cfg, sp)

        @block.tensor
        def _(pe):
            pe.wait_ge(k.aux_in, 16 * k.aux_n)
            for t in range(T):
                mm = nc.tensor.matmul(k.ps[:, 7, t * E:(t + 1) * E], src[:, t * P:(t + 1) * P], a["router"],
                                      start=True, stop=True)
            mm.then_inc(s_mm, 1)

        @block.scalar
        def _(act):
            nc.scalar.activation(k.xh, src, ACT.Copy).then_inc(s_xh, 1)
            act.wait_ge(s_xh, 1)
            nc.scalar.activation(k.xs, k.xh, ACT.Copy, scale=1.0 / Weights.LIFT)
            if not loaded:
                weights.make_hi(nc, act, 0)
            weights.make_hi(nc, act, 1)
            act.wait_ge(s_arg, 1)
            nc.scalar.activation(w, w, ACT.Exp, scale=-1.0 if kind == "sigmoid" else 1.0).then_inc(s_exp, 1)
            if kind == "softmax_all":
                nc.scalar.activation(eq, eq, ACT.Exp).then_inc(s_exp, 1)

        @block.vector
        def _(dve):
            st = k.dve_steps
            dve.wait_ge(s_xh, 1)
            st.inc(nc.vector.tensor_tensor(k.xl, src, k.xh, ALU.subtract))
            dve.wait_ge(s_mm, 1)
            ps = k.ps[:, 7, 0:T * E].rearrange("p (t e) -> p t e", e=E)
            def bias():
                return a["router_bias"].unsqueeze(1).to_broadcast([P, T, E])
            if kind == "softmax_all":
                st.link(dve, nc.vector.tensor_tensor(L, ps, bias(), ALU.add))
            else:
                st.link(dve, nc.vector.tensor_copy(L, ps))
            pick = L
            if kind == "sigmoid":
                st.link(dve, nc.vector.tensor_tensor(Lb, L, bias(), ALU.add))
                pick = Lb
            for t in range(T):
                st.inc(nc.vector.max(top[:, t, :], pick[:, t, :]))
            dve.wait_ge(st.sem, st.n)
            for t in range(T):
                st.inc(nc.vector.max_index(idx_i[:, t, :], top[:, t, :], pick[:, t, :]))
            dve.wait_ge(st.sem, st.n)
            st.link(dve, nc.vector.tensor_copy(idx, idx_i))

            def onehot(j):
                st.link(dve, nc.vector.tensor_tensor(eq, k.iota[:, 0:E].unsqueeze(1).to_broadcast([P, T, E]),
                                                     idx[:, :, j:j + 1].to_broadcast([P, T, E]), ALU.is_equal))
            if kind == "sigmoid":
                for j in range(K):
                    onehot(j)
                    st.link(dve, nc.vector.tensor_tensor(tmp, eq, L, ALU.mult))
                    st.link(dve, nc.vector.tensor_reduce(w[:, :, j:j + 1].rearrange("p t j -> p (t j)"), tmp, X_AXIS, ALU.add))
                nc.vector.memset(one, 0.0).then_inc(s_arg, 1)
                dve.wait_ge(s_exp, 1)
                st.link(dve, nc.vector.tensor_scalar(w, w, 1.0, None, ALU.add))
                st.link(dve, nc.vector.reciprocal(w, w))
                guard, floor = ALU.add, 1e-6
            else:
                if kind == "softmax_all":
                    st.link(dve, nc.vector.tensor_tensor(eq, L, top[:, :, 0:1].to_broadcast([P, T, E]), ALU.subtract))
                nc.vector.tensor_tensor(w, top[:, :, 0:K], top[:, :, 0:1].to_broadcast([P, T, K]), ALU.subtract).then_inc(s_arg, 1)
                guard, floor = None, None
                dve.wait_ge(s_exp, 1)
                if kind == "softmax_all":
                    dve.wait_ge(s_exp, 2)
                    st.link(dve, nc.vector.tensor_reduce(one, eq, X_AXIS, ALU.add))
                    st.link(dve, nc.vector.reciprocal(one, one))
                    st.link(dve, nc.vector.tensor_tensor(w, w, one.unsqueeze(2).to_broadcast([P, T, K]), ALU.mult))
                    guard, floor = cfg["guard"]
            st.link(dve, nc.vector.tensor_reduce(one, w, X_AXIS, ALU.add))
            if guard is not None:
                st.link(dve, nc.vector.tensor_scalar(one, one, floor, None, guard))
            st.link(dve, nc.vector.reciprocal(one, one))
            st.link(dve, nc.vector.tensor_tensor(w, w, one.unsqueeze(2).to_broadcast([P, T, K]), ALU.mult))
            if cfg["E"] > E:
                st.inc(nc.vector.memset(k.G[:, :, E:cfg["E"]], 1.0))
            for j in range(K):
                onehot(j)
                wj = w[:, :, j:j + 1].to_broadcast([P, T, E])
                if j == 0:
                    ins = nc.vector.tensor_tensor(G, eq, wj, ALU.mult)
                else:
                    st.link(dve, nc.vector.tensor_tensor(tmp, eq, wj, ALU.mult))
                    ins = nc.vector.tensor_tensor(G, G, tmp, ALU.add)
                if j < K - 1:
                    st.link(dve, ins)


def moe(nc, k, cfg):
    tag, E, nf, kind = cfg["tag"], cfg["E"], cfg["nf"], cfg["kind"]
    nub = cfg["nub"]
    R = 2 if E % 2 == 0 else 3
    nU = 4 if R == 2 else 3
    a = aux_views(k, cfg["aux"])
    gate_col = cfg["gate_col"]
    H = [k.P4[:, i * nf * CH:(i + 1) * nf * CH].rearrange("p (f n) -> p f n", f=nf) for i in range(R)]
    SG = [k.P4[:, (R + i) * CH:(R + i + 1) * CH] for i in range(R)] if kind in ("swiglu", "relu2") else None
    acc = k.acc[:, :].rearrange("p (t d) -> p t d", t=TC)
    Rs = [k.misc[:, i * CH:(i + 1) * CH].rearrange("p (t d) -> p t d", t=TC) for i in range(2)]
    xb = [k.misc[:, (2 + i) * CH:(3 + i) * CH].rearrange("p (t d) -> p t d", t=TC) for i in range(2)]
    fst = [k.small[:, 32 * i:32 * i + 24].rearrange("p (t s) -> p t s", t=TC) for i in range(2)]
    fmv = [k.small[:, 64 + 8 * i:72 + 8 * i].rearrange("p (t s) -> p t s", t=TC) for i in range(2)]
    fvar = [k.small[:, 80 + 4 * i:84 + 4 * i] for i in range(2)]
    frs = [k.small[:, 88 + 4 * i:92 + 4 * i] for i in range(2)]
    fw = [k.small[:, 96 + 4 * i:100 + 4 * i] for i in range(2)]
    mhalf = k.small[:, 104:108]
    s_up, s_act, s_h, s_dn, s_cb, s_xb, s_R, s_var, s_rs, s_ser = [k.sem(f"{tag}_{n}") for n in
        ("up", "act", "hidden", "down", "combined", "residual", "summed", "var", "rstd", "serial")]

    weights = cfg["weights"]
    has_bias_rows = "bias_rows" in a
    gT = k.V[0:E, 0:N]
    s_tp, s_ev, s_b, s_bc = [k.sem(f"{tag}_b_{n}") for n in ("gates_tp", "gates_T", "product", "copied")] if has_bias_rows else [None] * 4

    def quarter(c, e, late):
        return e - late if has_bias_rows and isinstance(c, int) and 0 <= e - late < 4 else None

    def chunks(eng, body):
        body(0)
        with eng.Fori(1, NC_) as c:
            body(c)

    first = lambda c: isinstance(c, int)

    def split_at(e):
        return [p for p in range(2, weights.pieces) if (p - 2) * weights.experts == e]

    with nc.Block() as block:
        @block.sync
        def _(sp):
            for p in range(2, weights.pieces):
                weights.load(sp, p)

        @block.tensor
        def _(pe):
            def chunk(c):
                for e in range(E + 1):
                    if e < E:
                        if first(c) and any(e == E * q // 4 for q in range(4)):
                            pe.wait_ge(k.w_in[[E * q // 4 for q in range(4)].index(e)], 16 * k.w_n)
                        if first(c) and e % weights.experts == 0:
                            pe.wait_ge(weights.s_done, e // weights.experts + 1)
                        for f in range(nub):
                            i = e * nub + f
                            if not (first(c) and i < nU):
                                if kind == "swiglu":
                                    pe.wait_ge((s_act, s_h)[f], c * E + e - 1)
                                elif kind == "relu2":
                                    pe.wait_ge(s_act, c * E + e - 2)
                                else:
                                    pe.wait_ge(s_act, c * (E * nub) + i - nU + 1)
                            cols = weights.up_cols(e, f)
                            terms = ((weights.hi, k.xh), (weights.hi, k.xl), (weights.lo, k.xs))
                            for n, (w, x) in enumerate(terms):
                                mm = nc.tensor.matmul(k.ps[:, i % nU, :], w[:, cols], x[:, bass.ds(c * CH, CH)],
                                                      start=(n == 0), stop=(n == 2))
                            mm.then_inc(s_up, 1)
                    q = quarter(c, e, 1)
                    if q is not None:
                        if q:
                            pe.wait_ge(s_ev, q)
                        for t in range(TC):
                            mm = nc.tensor.transpose(k.ps[0:E, 6, t * P:(t + 1) * P], k.G[:, q * TC + t, 0:E], k.ident[:, :])
                        mm.then_inc(s_tp, 1)
                    q = quarter(c, e, 2)
                    if q is not None:
                        pe.wait_ge(s_ev, q + 1)
                        if q:
                            pe.wait_ge(s_bc, q)
                        for t in range(TC):
                            mm = nc.tensor.matmul(k.ps[:, 7, t * P:(t + 1) * P], gT[:, q * CH + t * P:q * CH + (t + 1) * P],
                                                  a["bias_rows"][0:E, :], start=True, stop=True)
                        mm.then_inc(s_b, 1)
                    if e:
                        o, hb = (e - 1) % R, H[(e - 1) % R]
                        if kind in ("swiglu", "relu2"):
                            pe.wait_ge(s_h, c * E + e)
                        else:
                            pe.wait_ge(s_act, c * (E * nub) + e * nub)
                        if not (first(c) and e - 1 < R):
                            pe.wait_ge(s_cb, c * E + e - R)
                        for tt in range(TC):
                            for f in range(nf):
                                mm = nc.tensor.matmul(k.ps[:, 4 + o, tt * P:(tt + 1) * P], hb[:, f, tt * P:(tt + 1) * P],
                                                      weights.down(e - 1, f), start=(f == 0), stop=(f == nf - 1))
                        mm.then_inc(s_dn, 1)
            chunks(pe, chunk)

        @block.scalar
        def _(act):
            def chunk(c):
                for e in range(E):
                    if kind in ("swiglu", "relu2"):
                        act.wait_ge(s_up, c * (E * nub) + e * nub + 1)
                        if not (first(c) and e < R):
                            act.wait_ge(s_h, c * E + e - R + 1)
                        nc.scalar.activation(SG[e % R], k.ps[:, (e * nub) % nU, :],
                                             ACT.Silu if kind == "swiglu" else ACT.Relu).then_inc(s_act, 1)
                    else:
                        if not (first(c) and e < R):
                            act.wait_ge(s_dn, c * E + e - R + 1)
                        for f in range(nf):
                            i = e * nub + f
                            act.wait_ge(s_up, c * (E * nub) + i + 1)
                            nc.scalar.activation(H[e % R][:, f, :], k.ps[:, i % nU, :], ACT.Gelu,
                                                 bias=a["b1"][:, e * nf + f:e * nf + f + 1]).then_inc(s_act, 1)
                        q = quarter(c, e, 1)
                        if q is not None:
                            act.wait_ge(s_tp, q + 1)
                            nc.scalar.activation(gT[:, q * CH:(q + 1) * CH], k.ps[0:E, 6, :], ACT.Copy).then_inc(s_ev, 1)
                        q = quarter(c, e, 2)
                        if q is not None:
                            act.wait_ge(s_b, q + 1)
                            nc.scalar.activation(k.attn[:, q * TC:(q + 1) * TC, :], k.ps[:, 7, :].rearrange(
                                "p (t d) -> p t d", d=D), ACT.Copy).then_inc(s_bc, 1)
            chunks(act, chunk)

        @block.gpsimd
        def _(pool):
            if kind != "gelu_ln":
                for p in range(2, weights.pieces):
                    weights.split(nc, pool, p)
                return
            nc.gpsimd.memset(mhalf, -0.5).then_inc(s_ser, 1)
            pool.wait_ge(s_ser, 1)

            def chunk(c):
                def residual(e):
                    if not (first(c) and e < 2):
                        pool.wait_ge(s_R, c * E + e - 1)
                        nc.gpsimd.tensor_tensor(k.pjunk[:, e:e + 1], k.consts[:, 0:1], k.consts[:, 0:1], ALU.add)
                    nc.gpsimd.tensor_tensor(xb[e % 2], k.xn[:, bass.ds(c * TC, TC), :],
                                            a["b2"][:, e * D:(e + 1) * D].unsqueeze(1).to_broadcast([P, TC, D]),
                                            ALU.add).then_inc(s_xb, 1)
                residual(0)
                for e in range(E):
                    if first(c):
                        for p in split_at(e):
                            weights.split(nc, pool, p)
                    if e + 1 < E:
                        residual(e + 1)
                    pool.wait_ge(s_var, c * E + e + 1)
                    nc.gpsimd.tensor_tensor(frs[e % 2], fvar[e % 2], mhalf, ALU.pow).then_inc(s_rs, 1)
            chunks(pool, chunk)

        @block.vector
        def _(dve):
            st = Steps(s_ser)
            st.n = 1 if kind == "gelu_ln" else 0
            base = st.n
            size = []

            def chunk(c):
                if not first(c):
                    st.n = c * size[0] + base

                def hidden(e):
                    dve.wait_ge(s_act, c * E + e + 1)
                    if kind == "swiglu":
                        dve.wait_ge(s_up, c * (E * nub) + (e + 1) * nub)
                    if not (first(c) and e < R):
                        dve.wait_ge(s_dn, c * E + e - R + 1)
                    other = k.ps[:, (e * nub + 1) % nU, :] if kind == "swiglu" else SG[e % R]
                    nc.vector.tensor_tensor(H[e % R][:, 0, :], SG[e % R], other, ALU.mult).then_inc(s_h, 1)

                def combine(e):
                    dve.wait_ge(s_dn, c * E + e + 1)
                    if e:
                        dve.wait_ge(s_cb, c * E + e)
                    for tt in range(TC):
                        g = k.G[:, bass.ds(c * TC + tt, 1), gate_col(e)].rearrange("p t e -> p (t e)")
                        o = k.ps[:, 4 + e % R, tt * P:(tt + 1) * P]
                        if e == 0:
                            ins = nc.vector.tensor_scalar(acc[:, tt, :], o, g, None, ALU.mult)
                        else:
                            ins = nc.vector.scalar_tensor_tensor(acc[:, tt, :], o, g, acc[:, tt, :], ALU.mult, ALU.add)
                        if tt < TC - 1:
                            st.inc(ins)
                    ins.then_inc(s_cb, 1)

                def stats(e):
                    dve.wait_ge(s_dn, c * E + e + 1)
                    dve.wait_ge(s_xb, c * E + e + 1)
                    nc.vector.tensor_tensor(Rs[e % 2], k.ps[:, 4 + e % R, :].rearrange("p (t d) -> p t d", t=TC), xb[e % 2],
                                            ALU.add).then_inc(s_R, 1)
                    dve.wait_ge(s_R, c * E + e + 1)
                    for tt in range(TC):
                        ins = nc.vector.bn_stats(fst[e % 2][:, tt, :], Rs[e % 2][:, tt, :])
                    ins.then_inc(s_cb, 1)
                    dve.wait_ge(s_cb, c * E + e + 1)
                    nc.vector.memset(k.junk[:, e:e + 1], 0.0)
                    for tt in range(TC):
                        ins = nc.vector.bn_aggr(fmv[e % 2][:, tt, :], fst[e % 2][:, tt, :])
                    st.link(dve, ins)
                    nc.vector.tensor_scalar(fvar[e % 2], fmv[e % 2][:, :, 1], 1e-6, None, ALU.add).then_inc(s_var, 1)

                def normed(e):
                    dve.wait_ge(s_rs, c * E + e + 1)
                    g = k.G[:, bass.ds(c * TC, TC), gate_col(e)].rearrange("p t e -> p (t e)")
                    st.link(dve, nc.vector.tensor_tensor(fw[e % 2], frs[e % 2], g, ALU.mult))
                    for tt in range(TC):
                        ins = nc.vector.tensor_scalar(Rs[e % 2][:, tt, :], Rs[e % 2][:, tt, :], fmv[e % 2][:, tt, 0:1],
                                                      fw[e % 2][:, tt:tt + 1], ALU.subtract, ALU.mult)
                    st.link(dve, ins)
                    gam = a["gamma"][:, e * D:(e + 1) * D].unsqueeze(1).to_broadcast([P, TC, D])
                    if e == 0:
                        ins = nc.vector.tensor_tensor(acc, Rs[e % 2], gam, ALU.mult)
                    else:
                        st.link(dve, nc.vector.tensor_tensor(Rs[e % 2], Rs[e % 2], gam, ALU.mult))
                        ins = nc.vector.tensor_tensor(acc, acc, Rs[e % 2], ALU.add)
                    st.link(dve, ins)

                for e in range(E + 1):
                    if kind == "gelu_ln":
                        if e < E:
                            stats(e)
                        if e:
                            normed(e - 1)
                    elif kind == "gelu":
                        if e < E:
                            combine(e)
                    else:
                        if e < E:
                            hidden(e)
                        if e:
                            combine(e - 1)
                dve.wait_ge(s_cb, c * E + E)
                tiles = lambda buf: buf[:, bass.ds(c * TC, TC), :]
                if has_bias_rows:
                    if first(c):
                        dve.wait_ge(s_bc, 4)
                    st.link(dve, nc.vector.tensor_tensor(acc, acc, tiles(k.attn), ALU.add))
                if kind == "gelu":
                    st.link(dve, nc.vector.scalar_tensor_tensor(acc, acc, 0.3, tiles(k.xn), ALU.mult, ALU.add))
                gi = cfg["tanh"]
                st.link(dve, nc.vector.scalar_tensor_tensor(tiles(k.x), acc, k.tanh_g[:, gi:gi + 1], tiles(k.x),
                                                            ALU.mult, ALU.add))
                if first(c):
                    size.append(st.n - base)
            chunks(dve, chunk)


def slot(e):
    return slice(e, e + 1)


CFG0 = dict(tag="l0f", E=8, route_E=8, K=2, nf=4, nub=4, piece=2, kind="gelu_ln", route="softmax_top", tanh=1,
            src=lambda k: k.xnT[:, :], gate_col=slot,
            aux=[("router", 8), ("b1", 32), ("gamma", 8 * D), ("b2", 8 * D), ("bias_rows", D)])
CFG1 = dict(tag="l1f", E=36, route_E=32, K=4, nf=1, nub=2, piece=4, kind="swiglu", route="softmax_all", tanh=3,
            guard=(ALU.max, 1e-12), src=lambda k: k.xnT[:, :], gate_col=slot,
            aux=[("router", 32), ("router_bias", 32)])
CFG2 = dict(tag="l2f", E=8, route_E=8, K=2, nf=2, nub=2, piece=4, kind="gelu", route="softmax_all", tanh=5,
            guard=(ALU.add, 1e-8), src=lambda k: k.xnT[:, :], gate_col=slot,
            aux=[("router", 8), ("router_bias", 8), ("b1", 16), ("bias_rows", D)])
CFG3 = dict(tag="l3f", E=9, route_E=8, K=2, nf=1, nub=1, piece=3, kind="relu2", route="sigmoid", tanh=7,
            src=lambda k: k.xnT[:, :], gate_col=slot,
            aux=[("router", 8), ("router_bias", 8)])


def ffn(cfg):
    def stage(nc, k, loaded=True):
        if not loaded:
            cfg["weights"] = Weights(k, cfg)
        route(nc, k, cfg, loaded)
        moe(nc, k, cfg)
    return stage



NHEAD = 16


class Split:

    def __init__(self, k, tag, n_q, n_all, bias_q, bias_k, sign_q, sign_k, dest):
        self.k, self.n, self.dest = k, n_all, dest
        self.late_ring = 4
        self.q = n_q
        self.bias, self.sign = (bias_q, bias_k), (sign_q, sign_k)
        self.s_mm, self.s_hi, self.s_out, self.s_sb = (k.sem(f"{tag}_{n}") for n in ("proj", "split_hi", "split", "signed_bias"))
        self.hi = k.hi

    def side(self, i):
        return 0 if i < self.q else 1

    ring = lambda self, i: self.late_ring if i >= self.q else 4

    def bank(self, i):
        return self.k.ps[:, i % self.ring(i), :]

    def tensor_ready(self, pe, i):
        if i >= 4:
            pe.wait_ge(self.s_out, max(i - self.ring(i) + 1, self.q if self.ring(i) < 4 else 0))

    def scalar(self, nc, act, i):
        act.wait_ge(self.s_mm, i + 1)
        if i >= 2:
            act.wait_ge(self.s_out, i - 1)
        b = self.bias[self.side(i)]
        hi = self.hi[:, i % 2, :]
        if b is None:
            nc.scalar.activation(hi, self.bank(i), ACT.Copy).then_inc(self.s_hi, 1)
        else:
            if i == 0:
                act.wait_ge(self.s_sb, 2)
            nc.scalar.activation(hi, self.bank(i), ACT.Identity, bias=b(self.k.signed_bias, i),
                                 scale=self.sign[self.side(i)]).then_inc(self.s_hi, 1)

    def vector(self, nc, dve, i):
        dve.wait_ge(self.s_hi, i + 1)
        b = self.bias[self.side(i)]
        if b is None:
            ins = nc.vector.scalar_tensor_tensor(self.dest(i), self.hi[:, i % 2, :], self.sign[self.side(i)], self.bank(i),
                                                 ALU.mult, ALU.add)
        else:
            ins = nc.vector.scalar_tensor_tensor(self.dest(i), self.bank(i), b(self.biases, i), self.hi[:, i % 2, :],
                                                 ALU.add, ALU.add)
        ins.then_inc(self.s_out, 1)

    def sign_biases(self, nc, dve, biases):
        self.biases = biases
        for side in (0, 1):
            cols = slice(4 * side, 4 * side + 4)
            nc.vector.tensor_scalar(self.k.signed_bias[:, cols], biases[:, cols], self.sign[side], None,
                                    ALU.mult).then_inc(self.s_sb, 1)


def key_groups(cfg):
    return 1 if cfg["mqa"] else 4


def attention(nc, k, cfg):
    tag, kd, dv, scale, mqa = cfg["tag"], cfg["kd"], cfg["dv"], cfg["scale"], cfg["mqa"]
    src_q, src_k = k.xnT, (k.xnT if cfg["self"] else k.ctxT)
    wq = k.w[tag + "_q"]
    wk = k.w[tag + "_k"]
    wv = k.w[tag + "_v"] if tag + "_v" in k.w else None
    bias = k.w.get(tag + "_b")
    bv = k.w.get(tag + "_bv")
    KG = key_groups(cfg)
    VH = 1 if mqa else NHEAD
    nq, nk = 16, KG * NC_
    V = k.V[:, 0:T * VH * (dv + 1)].rearrange("p (t h e) -> p t h e", t=T, h=VH)
    KZ = k.big[:, :].bitcast(F16).rearrange("p (g j n) -> p g j n", g=4, j=HG)
    Prb = [k.P4[:, i * 1024:(i + 1) * 1024].rearrange("p (j t q) -> p j t q", j=2, t=2) for i in range(4)]
    mx = k.small[:, 0:16].rearrange("p (r t j) -> p r t j", r=2, t=2)
    c0 = 0 if kd == 8 else 2
    qdest = lambda i: k.Qs[:, i // NC_, (i % NC_) * CH:(i % NC_ + 1) * CH]
    kdest = lambda i: k.Kst[:, ((i - nq) // NC_) % 2, ((i - nq) % NC_) * CH:((i - nq) % NC_ + 1) * CH]
    sp_ = Split(k, tag, nq, nq + nk, (lambda cols, i: cols[:, i // NC_:i // NC_ + 1]) if bias is not None else None,
                (lambda cols, i: cols[:, 4 + (i - nq) // NC_:5 + (i - nq) // NC_]) if bias is not None else None,
                k.consts[:, c0:c0 + 1], k.consts[:, c0 + 1:c0 + 2], lambda i: qdest(i) if i < nq else kdest(i))
    s_const, s_v, s_vc, s_ones = [k.sem(f"{tag}_{n}") for n in ("k_constants", "v", "v_copied", "ones")]
    s_place = [k.sem(f"{tag}_k_placed{n}") for n in range(2)]
    sel = cfg.get("select")
    if sel:
        hooks = sel(nc, k, cfg, sp_, V)
    with nc.Block() as block:
        @block.gpsimd
        def _(pool):
            nc.gpsimd.memset(V[:, :, :, dv:dv + 1], 1.0).then_inc(s_ones, 1)
            pool.wait_ge(s_ones, 1)
            pairs = k.big[:, :].rearrange("p (g j n) -> p g j n", g=4, j=HG)
            for j in range(HG):
                nc.gpsimd.memset(pairs[BLK * j:BLK * j + 2, 0:KG, j, :], SHIFT_PAIR).then_inc(s_const, 1)

        @block.tensor
        def _(pe):
            for i in range(nq):
                g, c = divmod(i, NC_)
                sp_.tensor_ready(pe, i)
                nc.tensor.matmul(sp_.bank(i), wq[:, g * P:(g + 1) * P], src_q[:, c * CH:(c + 1) * CH], start=True,
                                 stop=True).then_inc(sp_.s_mm, 1)
            if sel:
                hooks["pe"](pe)
                return
            for i in range(nq, nq + nk):
                g, c = divmod(i - nq, NC_)
                sp_.tensor_ready(pe, i)
                nc.tensor.matmul(sp_.bank(i), wk[:, g * P:(g + 1) * P], src_k[:, c * CH:(c + 1) * CH], start=True,
                                 stop=True).then_inc(sp_.s_mm, 1)
            nv = VH * dv
            for t in range(T):
                if t % TC == 0 and t >= 3 * TC:
                    pe.wait_ge(s_vc, t // TC - 2)
                o = k.ps[:, 4 + (t // TC) % 3, (t % TC) * P:(t % TC) * P + nv]
                mm = nc.tensor.matmul(o, src_k[:, t * P:(t + 1) * P], wv[:, 0:nv], start=True, stop=bv is None)
                if bv is not None:
                    mm = nc.tensor.matmul(o, k.w["ones"][0:1, :], bv[0:1, 0:nv], start=False, stop=True)
                mm.then_inc(s_v, 1)

        @block.scalar
        def _(act):
            for i in range(nq):
                sp_.scalar(nc, act, i)
            if sel:
                hooks["act"](act)
                return
            for i in range(nq, nq + nk):
                sp_.scalar(nc, act, i)
            act.wait_ge(s_ones, 1)
            for q in range(NC_):
                act.wait_ge(s_v, TC * (q + 1))
                pv = k.ps[:, 4 + q % 3, :].rearrange("p (t n) -> p t n", t=TC)
                for t in range(TC):
                    ins = nc.scalar.activation(V[:, TC * q + t, :, 0:dv], pv[:, t, 0:VH * dv].rearrange("p (h e) -> p h e", h=VH), ACT.Copy)
                ins.then_inc(s_vc, 1)

        @block.vector
        def _(dve):
            if bias is not None:
                sp_.sign_biases(nc, dve, bias)
            for i in range(nq):
                sp_.vector(nc, dve, i)
            if sel:
                hooks["dve"](dve)
                return
            for i in range(nq, nq + nk):
                if i - nq >= 2 * NC_ and (i - nq) % NC_ == 0:
                    dve.wait_ge(s_place[(i - nq) // NC_ % 2], 16 * HG * ((i - nq) // NC_ // 2))
                sp_.vector(nc, dve, i)

        @block.sync
        def _(sp):
            sp.wait_ge(s_const, HG)
            for g in range(KG):
                sp.wait_ge(sp_.s_out, nq + NC_ * (g + 1))
                for j in range(HG):
                    r = slice(BLK * j + 2, BLK * j + BLK)
                    sp.dma_start(KZ[r, g, j, :], k.Kst[r, g % 2, :]).then_inc(s_place[g % 2], 16)
            for g in range(min(KG, 2)):
                sp.wait_ge(s_place[g], 16 * HG * (KG // 2 if KG > 1 else 1))

    s_mx, s_rd, s_hi, s_nm, s_mt, s_qa, s_st, s_ex, s_pv, s_no, s_rc, s_oc, s_oz, s_vg = [k.sem(f"{tag}_{n}") for n in
        ("max_scores", "maxima", "max_hi", "max_parts", "turned", "q_shifted", "scores_T", "probs", "out", "normed",
         "recip", "out_copied", "out_zeroed", "v_staged")]
    MT = k.ps[:, 7, 0:P].bitcast(F16)
    OUTT = k.ps[:, 6, 0:S]
    OT = k.OT
    GH = 1 if mqa else HG
    VG = [k.small[:, 128 + 80 * i:128 + 80 * i + 2 * GH * (dv + 1)].rearrange("p (t j e) -> p t j e", t=2, j=GH) for i in range(2)]
    TP = k.ps[:, 7, S:2 * S].rearrange("p (t j r) -> p t j r", t=2, r=BLK)
    rs = k.small[:, 16:24].rearrange("p (t j) -> p t j", t=2)
    kz_g = (lambda g: 0) if mqa else (lambda g: g)

    def back(b, g, by):
        return (b, g - by) if g >= by else (b - 1, g + 4 - by)

    def live(b):
        return not (isinstance(b, int) and (b < 0 or b >= B))

    def early(b, g, j):
        return isinstance(b, int) and 4 * b + g < j

    def sweep(eng, step):
        for g in range(4):
            step(0, g)
        with eng.Fori(1, B) as b:
            for g in range(4):
                step(b, g)
        for g in range(3):
            step(B, g)

    with nc.Block() as block:
        @block.gpsimd
        def _(pool):
            def step(b, g):
                if not live(b):
                    return
                if not early(b, g, 2):
                    pool.wait_ge(s_pv, 8 * b + 2 * g - 2)
                    nc.gpsimd.tensor_tensor(k.pjunk[:, g:g + 1], k.consts[:, 0:1], k.consts[:, 0:1], ALU.add)
                nc.gpsimd.tensor_copy(VG[g % 2], V[:, bass.ds(2 * b, 2), 0:1 if mqa else NHEAD, :][:, :, 0 if mqa else 4 * g:1 if mqa else 4 * g + 4, :]
                                      ).then_inc(s_vg, 1)
            sweep(pool, step)

        @block.tensor
        def _(pe):
            def max_scores(b, g, js):
                for j in js:
                    if not (early(b, g, 1) and j < 2):
                        pe.wait_ge(s_rd, 16 * b + 4 * g + j - 1)
                    for t in range(2):
                        mm = nc.tensor.matmul(k.ps[:, j % 2, t * S:(t + 1) * S], k.Qs[:, g, bass.ds(b * S + t * P, P)],
                                              KZ[:, kz_g(g), j, bass.ds(b * S, S)], start=True, stop=True)
                    mm.then_inc(s_mx, 1)

            def turn(b, g):
                b1, g1 = back(b, g, 1)
                b3, g3 = back(b, g, 3)
                if live(b1):
                    pe.wait_ge(s_nm, 4 * b1 + g1 + 1)
                    if not early(b1, g1, 1):
                        pe.wait_ge(s_qa, 4 * b1 + g1)
                if live(b3):
                    pe.wait_ge(s_oc, 4 * b3 + g3 + 1)
                    if not early(b3, g3, 1):
                        pe.wait_ge(s_no, 4 * b3 + g3)
                if live(b1):
                    for t in range(2):
                        mm = nc.tensor.transpose(MT[:, t * P:(t + 1) * P], k.NM[:, g1 % 2, t, :], k.identh[:, :])
                if live(b3):
                    for t in range(2):
                        mm = nc.tensor.transpose(k.ps[:, 7, S + t * P:S + (t + 1) * P], OT[:, g3 % 2, t * P:(t + 1) * P],
                                                 k.ident[:, :])
                if live(b1) or live(b3):
                    mm.then_inc(s_mt, 1)

            def scores_T(b, g, hc):
                if hc == 0:
                    pe.wait_ge(s_qa, 4 * b + g + 1)
                if not (early(b, g, 1)):
                    pe.wait_ge(s_ex, 8 * b + 2 * g + hc - 1)
                for jj in range(2):
                    for t in range(2):
                        mm = nc.tensor.matmul(k.ps[:, 2 + 2 * hc + jj, t * S:(t + 1) * S],
                                              KZ[:, kz_g(g), 2 * hc + jj, bass.ds(b * S + t * P, P)], k.Qaug[:, g % 2, :],
                                              start=True, stop=True)
                mm.then_inc(s_st, 1)

            def weigh(b, g, hc):
                pe.wait_ge(s_ex, 8 * b + 2 * g + hc + 1)
                if hc == 0:
                    if early(b, g, 1):
                        pe.wait_ge(s_oz, 1)
                    else:
                        pe.wait_ge(s_oc, 4 * b + g)
                    pe.wait_ge(s_vg, 4 * b + g + 1)
                pr = Prb[(2 * g + hc) % 4]
                for t in range(2):
                    for jj in range(2):
                        j = 2 * hc + jj
                        mm = nc.tensor.matmul(OUTT[BLK * j:BLK * j + dv + 1, :],
                                              VG[g % 2][:, t, 0 if mqa else j, :],
                                              pr[:, jj, t, :], start=(t == 0), stop=(t == 1), skip_group_check=True)
                mm.then_inc(s_pv, 1)

            def step(b, g):
                b1, g1 = back(b, g, 1)
                b2, g2 = back(b, g, 2)
                if live(b):
                    max_scores(b, g, (0, 1))
                turn(b, g)
                if live(b2):
                    weigh(b2, g2, 0)
                if live(b):
                    max_scores(b, g, (2, 3))
                if live(b1):
                    scores_T(b1, g1, 0)
                if live(b2):
                    weigh(b2, g2, 1)
                if live(b1):
                    scores_T(b1, g1, 1)
            sweep(pe, step)

        @block.scalar
        def _(act):
            def step(b, g):
                b1, g1 = back(b, g, 1)
                b2, g2 = back(b, g, 2)
                for hc in range(2):
                    if hc and live(b2):
                        act.wait_ge(s_pv, 8 * b2 + 2 * g2 + 2)
                        if not early(b2, g2, 2):
                            act.wait_ge(s_mt, 4 * b2 + g2 + 1)
                        nc.scalar.activation(OT[:, g2 % 2, :], OUTT, ACT.Copy).then_inc(s_oc, 1)
                    if not live(b1):
                        continue
                    act.wait_ge(s_st, 8 * b1 + 2 * g1 + hc + 1)
                    if not early(b1, g1, 2):
                        act.wait_ge(s_pv, 8 * b1 + 2 * g1 + hc - 3)
                    nc.scalar.activation(Prb[(2 * g1 + hc) % 4].rearrange("p j t q -> p (j t q)"),
                                         k.ps[:, 2 + 2 * hc:4 + 2 * hc, :].rearrange("p a b -> p (a b)"),
                                         ACT.Exp, scale=scale).then_inc(s_ex, 1)
            sweep(act, step)

        @block.vector
        def _(dve):
            def reduce(b, g, js):
                for j in js:
                    dve.wait_ge(s_mx, 16 * b + 4 * g + j + 1)
                    nc.vector.tensor_reduce(mx[:, g % 2, :, j], k.ps[:, j % 2, :].rearrange("p (t n) -> p t n", t=2),
                                            X_AXIS, ALU.max).then_inc(s_rd, 1)

            def parts(b, g):
                nm = k.NM[:, g % 2, :, :].rearrange("p t (j r) -> p t j r", r=BLK)
                dve.wait_ge(s_rd, 16 * b + 4 * g + 4)
                if not early(b, g, 2):
                    dve.wait_ge(s_mt, 4 * b + g - 1)
                nc.vector.tensor_scalar(nm[:, :, :, 0], mx[:, g % 2, :, :], -1.0 / SHIFT, None, ALU.mult).then_inc(s_hi, 1)
                dve.wait_ge(s_hi, 4 * b + g + 1)
                nc.vector.scalar_tensor_tensor(nm[:, :, :, 1], mx[:, g % 2, :, :], -1.0 / SHIFT, nm[:, :, :, 0],
                                               ALU.mult, ALU.subtract).then_inc(s_nm, 1)

            def shift_q(b, g):
                dve.wait_ge(s_mt, 4 * b + g + 1)
                if not early(b, g, 2):
                    dve.wait_ge(s_st, 8 * b + 2 * g - 2)
                nc.vector.tensor_tensor(k.Qaug[:, g % 2, :], MT, k.Qs[:, g, bass.ds(b * S, S)], ALU.add).then_inc(s_qa, 1)

            def normalise(b, g):
                dve.wait_ge(s_mt, 4 * b + g + 3)
                if not early(b, g, 1):
                    dve.wait_ge(s_no, 4 * b + g)
                nc.vector.reciprocal(rs, TP[:, :, :, dv]).then_inc(s_rc, 1)
                dve.wait_ge(s_rc, 4 * b + g + 1)
                at = k.attn[:, bass.ds(2 * b, 2), 4 * g * dv:4 * (g + 1) * dv].rearrange("p t (j e) -> p t j e", j=HG)
                nc.vector.tensor_tensor(at, TP[:, :, :, 0:dv], rs.unsqueeze(3).to_broadcast([P, 2, HG, dv]),
                                        ALU.mult).then_inc(s_no, 1)

            nc.vector.memset(OUTT, 0.0).then_inc(s_oz, 1)

            def step(b, g):
                b1, g1 = back(b, g, 1)
                b3, g3 = back(b, g, 3)
                if live(b):
                    reduce(b, g, (0, 1))
                if live(b1):
                    shift_q(b1, g1)
                if live(b3):
                    normalise(b3, g3)
                if live(b):
                    reduce(b, g, (2, 3))
                    parts(b, g)
            sweep(dve, step)
            if cfg.get("add") is not None:
                gi = cfg["add"]
                dve.wait_ge(s_no, 4 * B)
                nc.vector.scalar_tensor_tensor(k.x[:, :, :], k.attn[:, :, :], k.tanh_g[:, gi:gi + 1], k.x[:, :, :],
                                               ALU.mult, ALU.add)
    if cfg.get("finish"):
        cfg["finish"](nc, k, cfg)


def select_kv(nc, k, cfg, split, V):
    tag, KW = cfg["tag"], P + 8
    qpT = k.attn[:, :, :].rearrange("p t d -> p (t d)")
    kv = k.P4[:, 0:T * KW].rearrange("p (t n) -> p t n", n=KW)
    OHT = [k.P4[:, T * KW + i * 2 * S:T * KW + (i + 1) * 2 * S].rearrange("p (m l) -> p m l", m=2) for i in range(2)]
    OH = [k.misc[:, i * S:(i + 1) * S] for i in range(4)]
    top, idx = k.small[:, 64:72], k.small[:, 72:80]
    s_qf, s_qc, s_sc, s_oh, s_km, s_kc, s_tm, s_tc, s_mv, s_vc = [k.sem(f"{tag}_{n}") for n in
        ("qp", "qp_copied", "scores", "onehot", "kv", "kv_copied", "onehot_T", "onehot_T_copied", "mv", "mv_copied")]
    nq = split.q
    split.late_ring = 2

    def pe_part(pe):
        for c in range(NC_):
            nc.tensor.matmul(k.ps[:, 4 + c, :], k.w["l2x_full"][:, :], k.xnT[:, c * CH:(c + 1) * CH], start=True,
                             stop=True).then_inc(s_qf, 1)
        pe.wait_ge(s_qc, NC_)
        mv_at = lambda b, t: k.ps[:, 2 + b % 2, 8 * t:8 * t + 8]

        def pick(b):
            pe.wait_ge(s_oh, 2 * b + 2)
            if b:
                pe.wait_ge(s_tc, b)
            for m in range(2):
                for t in range(2):
                    mm = nc.tensor.transpose(k.ps[:, 6, m * S + t * P:m * S + (t + 1) * P],
                                             OH[(2 * b + t) % 4][:, m * P:(m + 1) * P], k.ident[:, :])
            mm.then_inc(s_tm, 1)
            pe.wait_ge(s_tc, b + 1)
            pe.wait_ge(s_kc, 2 * b + 2)
            i = nq + b // 2
            if b % 2 == 0:
                split.tensor_ready(pe, i)
            for m in range(2):
                mm = nc.tensor.matmul(split.bank(i)[:, (b % 2) * S:(b % 2 + 1) * S], kv[:, 2 * b + m, 0:P],
                                      OHT[b % 2][:, m, :], start=(m == 0), stop=(m == 1))
            if b % 2:
                mm.then_inc(split.s_mm, 1)
            if b >= 2:
                pe.wait_ge(s_vc, b - 1)
            for t in range(2):
                for m in range(2):
                    mm = nc.tensor.matmul(mv_at(b, t), OHT[b % 2][:, m, t * P:(t + 1) * P], kv[:, 2 * b + m, P:KW],
                                          start=(m == 0), stop=(m == 1))
            mm.then_inc(s_mv, 1)

        for t in range(T):
            if t >= 2:
                pe.wait_ge(s_oh, t - 1)
            b = t // 2
            nc.tensor.matmul(k.ps[:, 4 + t % 2, 0:S], qpT[:, t * P:(t + 1) * P], k.ctxT[:, b * S:(b + 1) * S],
                             start=True, stop=True).then_inc(s_sc, 1)
            if t:
                pe.wait_ge(s_kc, t)
            nc.tensor.matmul(k.ps[:, 7, 0:KW], k.ctxT[:, t * P:(t + 1) * P], k.w["l2x_k"][:, :], start=True,
                             stop=True).then_inc(s_km, 1)
            if t % 2 and t >= 3:
                pick((t - 3) // 2)
        pick(B - 1)

    def act_part(act):
        for c in range(NC_):
            act.wait_ge(s_qf, c + 1)
            nc.scalar.activation(qpT[:, c * CH:(c + 1) * CH], k.ps[:, 4 + c, :], ACT.Copy).then_inc(s_qc, 1)

        def pick(b):
            act.wait_ge(s_tm, b + 1)
            if b >= 2:
                act.wait_ge(s_mv, b - 1)
            nc.scalar.activation(OHT[b % 2].rearrange("p m l -> p (m l)"), k.ps[:, 6, :], ACT.Copy).then_inc(s_tc, 1)
            act.wait_ge(s_mv, b + 1)
            nc.scalar.activation(V[:, 2 * b:2 * b + 2, 0, 0:8], k.ps[:, 2 + b % 2, 0:16].rearrange(
                "p (t e) -> p t e", t=2), ACT.Copy).then_inc(s_vc, 1)
            if b % 2:
                split.scalar(nc, act, nq + b // 2)

        for t in range(T):
            act.wait_ge(s_km, t + 1)
            nc.scalar.activation(kv[:, t, :], k.ps[:, 7, 0:KW], ACT.Copy).then_inc(s_kc, 1)
            if t % 2 and t >= 3:
                pick((t - 3) // 2)
        pick(B - 1)

    def dve_part(dve):
        st = k.dve_steps
        idx_i = k.idx_i[:, 0:8]
        for t in range(T):
            dve.wait_ge(s_sc, t + 1)
            sc = k.ps[:, 4 + t % 2, 0:S]
            st.link(dve, nc.vector.max(top, sc))
            st.link(dve, nc.vector.max_index(idx_i, top, sc))
            st.link(dve, nc.vector.tensor_copy(idx, idx_i))
            if t >= 4:
                dve.wait_ge(s_tm, (t - 4) // 2 + 1)
            nc.vector.tensor_scalar(OH[t % 4], k.iota[:, :], idx[:, 0:1], None, ALU.is_equal).then_inc(s_oh, 1)
            dve.wait_ge(s_oh, t + 1)
            if t % 2 and t >= 5 and ((t - 3) // 2) % 2:
                split.vector(nc, dve, nq + (t - 3) // 4)
        split.vector(nc, dve, nq + (B - 1) // 2)

    return {"pe": pe_part, "act": act_part, "dve": dve_part}


def turn_attn(nc, k, width, dst, s_tp):
    def pe_part(pe):
        for t in range(T):
            nc.tensor.transpose(k.ps[0:width, t // TC, (t % TC) * P:(t % TC + 1) * P], k.attn[:, t, 0:width],
                                k.ident[:, :]).then_inc(s_tp, 1)

    def act_part(act, done):
        for c in range(NC_):
            act.wait_ge(s_tp, TC * (c + 1))
            nc.scalar.activation(dst[:, c * CH:(c + 1) * CH], k.ps[0:width, c, :], ACT.Copy).then_inc(done, 1)
    return pe_part, act_part


def project_out(nc, k, cfg):
    s_tp, s_cp, s_mm = [k.sem(f"{cfg['tag']}_o_{n}") for n in ("tp", "copied", "mm")]
    pe_turn, act_turn = turn_attn(nc, k, P, k.xnT, s_tp)
    with nc.Block() as block:
        @block.tensor
        def _(pe):
            pe_turn(pe)
            for t in range(T):
                if t % TC == 0:
                    pe.wait_ge(s_cp, t // TC + 1)
                nc.tensor.matmul(k.ps[:, 4 + t // TC, (t % TC) * P:(t % TC + 1) * P], k.xnT[:, t * P:(t + 1) * P],
                                 k.w["l2x_c"][:, :], start=True, stop=True).then_inc(s_mm, 1)

        @block.scalar
        def _(act):
            act_turn(act, s_cp)

        @block.vector
        def _(dve):
            for c in range(NC_):
                dve.wait_ge(s_mm, TC * (c + 1))
                xs = k.x[:, TC * c:TC * (c + 1), :]
                nc.vector.scalar_tensor_tensor(xs, k.ps[:, 4 + c, :].rearrange("p (t d) -> p t d", d=D),
                                               k.tanh_g[:, 4:5], xs, ALU.mult, ALU.add)


def project_latent(nc, k, cfg):
    s_tp, s_cp, s_mm = [k.sem(f"{cfg['tag']}_o_{n}") for n in ("tp", "copied", "mm")]
    LAT = NHEAD * cfg["dv"]
    aoT = k.V[0:LAT, 0:N]
    pe_turn, act_turn = turn_attn(nc, k, LAT, aoT, s_tp)
    with nc.Block() as block:
        @block.tensor
        def _(pe):
            pe_turn(pe)
            for c in range(NC_):
                pe.wait_ge(s_cp, c + 1)
                nc.tensor.matmul(k.ps[:, 4 + c, :], k.w["l2m_o"][0:LAT, :], aoT[:, c * CH:(c + 1) * CH], start=True,
                                 stop=True).then_inc(s_mm, 1)

        @block.scalar
        def _(act):
            act_turn(act, s_cp)
            for c in range(NC_):
                act.wait_ge(s_mm, c + 1)
                nc.scalar.activation(k.xnT[:, c * CH:(c + 1) * CH], k.ps[:, 4 + c, :], ACT.Identity,
                                     bias=k.w["l2m_ob"][:, 0:1])


A2 = dict(tag="l2x", kd=8, dv=8, scale=float(1 / np.sqrt(8.0)), mqa=True, self=False, select=select_kv, finish=project_out)
A2M = dict(tag="l2m", kd=4, dv=4, scale=0.5, mqa=False, self=True, finish=project_latent)
A1 = dict(tag="l1x", kd=8, dv=8, scale=float(1 / np.sqrt(8.0)), mqa=False, self=False, add=2)
A3 = dict(tag="l3x", kd=8, dv=8, scale=float(1 / np.sqrt(128.0)), mqa=False, self=False, add=6)


def attend(cfg):
    return lambda nc, k: attention(nc, k, cfg)



def program(nc, d, out, stages=99):
    with ExitStack() as ctx:
        k = Ctx()
        k.d = d
        k.ln_calls = 0

        def sb(name, shape, dt=F32):
            return ctx.enter_context(nc.sbuf_tensor(name, shape, dt))

        def sem(name):
            return ctx.enter_context(nc.semaphore(name))

        stage_sems = []

        def stage_sem(name):
            handle = nc.alloc_semaphore(name=name)
            stage_sems.append(handle)
            return handle

        def retire_stage_sems():
            with nc.Block() as block:
                @block.gpsimd
                def _(pool):
                    for handle in stage_sems:
                        nc.gpsimd.sem_clear(handle)
            for handle in stage_sems:
                nc.release_semaphore(handle)
            stage_sems.clear()

        k.sem = stage_sem
        k.x, k.xn = sb("x", [P, T, D]), sb("xn", [P, T, D])
        k.xnT, k.ctxT = sb("xnT", [P, N]), sb("ctxT", [P, N])
        k.attn = sb("attn", [P, T, D])
        k.V = sb("V", [P, T * 16 * 9])
        k.Qs = sb("Qs", [P, 4, N], F16)
        k.Kst = sb("Kst", [P, 2, N], F16)
        k.big = sb("big", [P, 16 * N // 2])
        k.P4 = sb("P4", [P, 4 * 1024])
        k.misc = sb("misc", [P, 2048])
        k.small = sb("small", [P, 512])
        k.zeros = sb("zeros", [P, S])
        k.Qaug = sb("Qaug", [P, 2, S], F16)
        k.OT = sb("OT", [P, 2, S])
        k.NM = sb("NM", [P, 2, 2, P], F16)
        k.stats, k.mv = sb("stats", [P, T, 6]), sb("mv", [P, T, 2])
        k.std, k.rstd = sb("std", [P, T]), sb("rstd", [P, T])
        k.ident, k.identh, k.identb = sb("ident", [P, P]), sb("identh", [P, P], F16), sb("identb", [P, P], BF16)
        k.cmask = sb("cmask", [P, S + P], BF16)
        k.sel32, k.sel = k.big[0:32, 0:32 * P], k.big[:, 0:32 * P]
        k.keys = k.big[:, 32 * P:32 * P + 4 * N]
        k.G = sb("G", [P, T, 36])
        k.idx_i = sb("idx_i", [P, 8 * T], U32)
        k.acc = sb("acc", [P, CH])
        k.aux = k.Qs[:, :, :].rearrange("p g n -> p (g n)").bitcast(F32)
        half = k.Kst[:, :, :]
        k.xh, k.xl = half[:, 0, :], half[:, 1, :]
        k.xs = k.Qs[:, 3, :]
        k.hi = sb("hi", [P, 2, CH], F16)
        k.junk, k.pjunk = sb("junk", [P, 8]), sb("pjunk", [P, 8])
        k.iota = sb("iota", [P, S])
        k.consts = sb("consts", [P, 8])
        k.signed_bias = sb("signed_bias", [P, 8])
        k.gates_raw, k.tanh_g = sb("gates_raw", [P, 8]), sb("tanh_g", [P, 8])
        k.ps = ctx.enter_context(nc.psum_tensor("ps", [P, 8, CH], F32))
        k.w = {n: sb("w_" + n, list(d[n].shape)) for n in SMALL_WEIGHTS}
        k.ln_var, k.ln_std, k.ln_xn, k.ln_tp = sem("ln_var"), sem("ln_std"), sem("ln_xn"), sem("ln_tp")
        k.setup_in, k.first_in, k.rest_in, k.sel_zero, k.ctx_tp, k.out_done = sem("setup_in"), sem("first_in"), sem("rest_in"), sem("sel_zero"), sem("ctx_tp"), sem("out_done")
        k.aux_in, k.w_in = sem("aux_in"), [sem(f"w_in{q}") for q in range(4)]
        k.aux_n = k.w_n = 0
        k.dve_steps, k.act_steps = Steps(sem("dve_steps")), Steps(sem("act_steps"))

        setup(nc, k)
        plan = STAGES[:stages]
        for n, (stage, groups, cfg) in enumerate(plan):
            if n and n % 4 == 0:
                retire_stage_sems()
            loads = (lambda sp: load_first(k, sp)) if n == 0 else None
            if cfg is not None:
                cfg["weights"] = Weights(k, cfg)
                loads = lambda sp, cfg=cfg: load_layer(nc, k, cfg, sp)
            layer_norm(nc, k, loads, groups * HG * N // 2, cfg["weights"] if cfg is not None else None)
            if n == 0:
                await_loads(nc, k.first_in, k.first_n)
            stage(nc, k)
            if n == 0:
                await_loads(nc, k.rest_in, k.rest_n)
        with nc.Block() as block:
            @block.sync
            def _(sp):
                sp.dma_start(out.rearrange("(t p) d -> p t d", p=P), k.x[:, :, :]).then_inc(k.out_done, 16)
                sp.wait_ge(k.out_done, 16)


SMALL_WEIGHTS = ["l0_gate", "l0_gbias", "l0_rms", "ones", "l1x_q", "l1x_k", "l1x_v", "l3x_q", "l3x_k", "l3x_v", "l3x_b", "l3x_bv",
                 "l2m_q", "l2m_k", "l2m_v", "l2m_b", "l2m_bv", "l2m_o", "l2m_ob", "l2x_q", "l2x_k", "l2x_full", "l2x_c"]
def latent_ffn(nc, k):
    attention(nc, k, A2M)
    ffn(CFG2)(nc, k, loaded=False)


STAGES = [(mlstm, 0, None), (ffn(CFG0), 0, CFG0), (attend(A1), key_groups(A1), None), (ffn(CFG1), 0, CFG1),
          (attend(A2), key_groups(A2), None), (latent_ffn, key_groups(A2M), None),
          (attend(A3), key_groups(A3), None), (ffn(CFG3), 0, CFG3)]



def constants():
    c = {}
    c["ident"] = np.eye(P, dtype=np.float32)
    c["identh"] = np.eye(P, dtype=np.float16)
    key, qry = np.arange(P)[:, None], np.arange(P)[None, :]
    tri = np.where(qry < key, NEG, 0.0)
    c["cmask"] = np.concatenate([tri, np.zeros((P, P)), tri], 1).astype(np.float32)
    c["iota"] = np.broadcast_to(np.arange(S, dtype=np.float32), (P, S)).copy()
    sel = np.zeros((32, 32, P), np.float32)
    sel[np.arange(32), np.arange(32)] = 1.0
    c["sel32"] = sel.reshape(32, 32 * P)
    cons = np.zeros((P, 8), np.float32)
    row = np.arange(P) % BLK - 2
    for i, (kd, lo) in enumerate(((8, 2), (8, 1), (4, 2), (4, 1))):
        cons[:, i] = np.where((row >= lo * kd) & (row < (lo + 1) * kd), -1.0, 0.0)
    c["consts"] = cons
    return c


def layouts(i):
    o = {}
    f = lambda a: np.ascontiguousarray(a, dtype=np.float32)
    o["x"], o["ctx"] = f(i["x"]).reshape(N, D), f(i["ctx_1024"]).reshape(N, D)
    g = np.stack([f(i["g_xattn"]), f(i["g_ffn"])], 1).reshape(1, 8)
    o["g_all"] = np.repeat(g, P, 0)
    w = np.zeros((P, 3, 92), np.float32)
    for n, name in enumerate(("igate", "fgate")):
        w[:, :, 28 + 32 * n:32 + 32 * n] = f(i[f"L0_xattn_{name}_kernel"]).reshape(3, D, 4).transpose(1, 0, 2)
    o["l0_gate"] = w.reshape(P, 3 * 92)
    b = np.zeros((P, 2), np.float32)
    for n, name in enumerate(("igate", "fgate")):
        b[0:32, n] = np.tile(f(i[f"L0_xattn_{name}_bias"]), 8)
    o["l0_gbias"] = b
    o["l0_rms"] = np.broadcast_to(np.tile(f(i["L0_xattn_rms_scale"]), 4), (P, D)).copy()
    def rows(a):
        return np.concatenate([f(a), np.zeros((P - a.shape[0], a.shape[1]), np.float32)], 0)

    def spread(a):
        return np.repeat(f(a).reshape(1, -1), P, 0)

    def hidden_cols(a):
        return f(a).reshape(-1, P).T

    def tile_rows(a):
        e, ff, dd = a.shape
        return f(a).reshape(e, ff // P, P, dd).transpose(2, 0, 1, 3).reshape(P, e, -1)

    def cat(*parts):
        return np.concatenate(parts, 2).reshape(P, -1)

    tr = lambda a: f(a).transpose(2, 0, 1)
    o["l0f_aux"] = np.concatenate([f(i["L0_ffn_router_w"]), hidden_cols(i["L0_ffn_b1"]), spread(i["L0_ffn_gamma"]),
                                   spread(i["L0_ffn_b2"]), rows(i["L0_ffn_beta"])], 1)
    o["l0f_up"], o["l0f_dn"] = cat(f(i["L0_ffn_w1"]).transpose(1, 0, 2)), cat(tile_rows(i["L0_ffn_w2"]))
    o["l1f_aux"] = np.concatenate([f(i["L1_ffn_router_w"]).T, spread(i["L1_ffn_router_bias"])], 1)
    four = lambda a: f(a).reshape(4, P, D)
    o["l1f_up"] = cat(*(np.concatenate([tr(x), tr(four(y))], 1) for x, y in (
        (i["L1_ffn_gate_w"], i["L1_ffn_sgate_w"]), (i["L1_ffn_up_w"], i["L1_ffn_sup_w"]))))
    o["l1f_dn"] = cat(np.concatenate([tr(i["L1_ffn_down_w"]),
                                      f(i["L1_ffn_sdown_w"]).T.reshape(4, P, D).transpose(1, 0, 2)], 1))
    o["l2f_aux"] = np.concatenate([f(i["L2_ffn_router_w"]), spread(i["L2_ffn_router_b"]), hidden_cols(i["L2_ffn_b1"]),
                                   rows(i["L2_ffn_b2"])], 1)
    o["l2f_up"], o["l2f_dn"] = cat(f(i["L2_ffn_w1"]).transpose(1, 0, 2)), cat(tile_rows(i["L2_ffn_w2"]))
    o["l3f_aux"] = np.concatenate([f(i["L3_ffn_gate_w"]).T, spread(i["L3_ffn_lb_bias"])], 1)
    o["l3f_up"], o["l3f_dn"] = [cat(np.concatenate([tr(x), f(y).T[:, None, :]], 1)) for x, y in (
        (i["L3_ffn_w1"], i["L3_ffn_cfc"]), (i["L3_ffn_w2"], i["L3_ffn_cproj"]))]

    def blocks(a, kd):
        a = f(a).reshape(a.shape[0], -1, kd)
        z = np.zeros(a.shape[:2] + (BLK,), np.float32)
        for r in range(3):
            z[:, :, 2 + r * kd:2 + (r + 1) * kd] = a
        return z.reshape(a.shape[0], -1)

    def bias_cols(q, kk, kd):
        return np.concatenate([blocks(np.asarray(v).reshape(1, -1), kd).reshape(-1, P).T for v in (q, kk)], 1)

    o["ones"] = np.ones((P, P), np.float32)
    o["l1x_q"], o["l1x_k"] = blocks(f(i["L1_xattn_Wq"]).T, 8), blocks(f(i["L1_xattn_Wk"]).T, 8)
    o["l1x_v"] = f(i["L1_xattn_Wv"]).T
    o["l3x_q"], o["l3x_k"], o["l3x_v"] = blocks(i["L3_xattn_Wq"], 8), blocks(i["L3_xattn_Wk"], 8), f(i["L3_xattn_Wv"])
    o["l3x_b"], o["l3x_bv"] = bias_cols(i["L3_xattn_bq"], i["L3_xattn_bk"], 8), spread(i["L3_xattn_bv"])
    four_of_8 = lambda a: f(a).reshape(-1, 16, 8)[:, :, 0:4].reshape(-1, 64)
    o["l2m_q"], o["l2m_k"], o["l2m_v"] = blocks(four_of_8(i["L2_ffn_q_w"]), 4), blocks(i["L2_ffn_k_w"], 4), f(i["L2_ffn_v_w"])
    o["l2m_b"], o["l2m_bv"] = bias_cols(four_of_8(i["L2_ffn_q_b"]), i["L2_ffn_k_b"], 4), spread(i["L2_ffn_v_b"])
    o["l2m_o"], o["l2m_ob"] = f(i["L2_ffn_o_w"]), f(i["L2_ffn_o_b"]).reshape(P, 1)
    wkv = f(i["L2_xattn_Wkv"]).T
    o["l2x_q"] = blocks(f(i["L2_xattn_Wq"]).T, 8)
    o["l2x_k"] = np.concatenate([blocks(np.tile(wkv[:, 0:8], (1, HG)), 8), wkv[:, 8:16]], 1)
    o["l2x_full"], o["l2x_c"] = f(i["L2_xattn_Wq"]).T, f(i["L2_xattn_Wc"]).T
    return o


def kernel(**inputs):
    import concourse.bacc as _bacc
    from concourse.bass_utils import run_bass_kernel_spmd as _run

    nc = _bacc.Bacc("TRN2", target_bir_lowering=False, num_devices=1)
    arrays, d = {}, {}
    for name, a in {**constants(), **layouts(inputs)}.items():
        a = np.ascontiguousarray(a)
        arrays[f"in_{name}"] = a
        d[name] = nc.dram_tensor(f"in_{name}", a.shape, mybir.dt.from_np(a.dtype), kind="ExternalInput").ap()
    out = nc.dram_tensor("out_x", (N, D), F32, kind="ExternalOutput").ap()
    program(nc, d, out)
    r = _run(nc, [arrays], core_ids=[0])
    return r.results[0]["out_x"].reshape(B, S, D)
```
